# Optimizing a Trainium2 kernel written in Bass

```python
import numpy as np
import jax
import jax.numpy as jnp

def _softmax(x, axis=-1):
    return jax.nn.softmax(x, axis=axis)
def _gelu(x):
    return jax.nn.gelu(x, approximate=True)
def _silu(x):
    return jax.nn.silu(x)
def _sigmoid(x):
    return jax.nn.sigmoid(x)
def _layernorm(x, axis=-1, eps=1e-5):
    m = jnp.mean(x, axis=axis, keepdims=True)
    v = jnp.var(x, axis=axis, keepdims=True)
    return (x - m) / jnp.sqrt(v + eps)
def _scatter_add(tgt, idx, src, axis=0):
    return tgt.at[idx].add(src)
def _segment_sum(src, seg, n):
    return jax.ops.segment_sum(src, seg, n)

kernel_name = 'mk_adj_preln_d2_adj_768_a32704'

def setup_inputs(seed: int = 0):
    np.random.seed(seed)
    _w = jnp.asarray
    def _rec_inputs():
        import jax
        import jax.numpy as jnp
        _gk = jax.random.key(seed)
        x = -0.0001538 + 1 * jax.random.normal(jax.random.fold_in(_gk, 1), (128, 64, 768), jnp.float32)
        _w = (1.0 + jnp.arange(64, dtype=jnp.float32)) ** -0.5
        _w = _w / _w.mean()
        _pij = jnp.clip(0.125 * _w[:, None] * _w[None, :], 0.0, 1.0)
        _a = jax.random.uniform(jax.random.fold_in(_gk, 2), (128, 64, 64)) < _pij
        _a = jnp.logical_or(_a, jnp.eye(64, dtype=bool))
        adj = _a
        return x, adj
    x, adj = _rec_inputs()
    def _L0_gnn_setup():
        import jax, jax.numpy as jnp
        import numpy as np
        B, S, H = (4, 2048, 768)
        NUM_HEADS = 6
        HEAD_SIZE = H // NUM_HEADS
        NEG = -9000000000000000.0

        def _heads(x):
            b, s, _ = x.shape
            return x.reshape(b, s, NUM_HEADS, HEAD_SIZE).transpose(0, 2, 1, 3)
        key = jax.random.key(seed)
        ks = jax.random.split(key, 10)
        seq_inputs = jax.random.normal(ks[0], (B, S, H), dtype=jnp.float32)
        gm = jax.random.randint(ks[1], (B, S, S), 0, 2) > 0
        graph_mask = gm | jnp.eye(S, dtype=bool)[None]
        sc = 1.0 / np.sqrt(H)
        Wq = jax.random.normal(ks[2], (H, H), dtype=jnp.float32) * sc
        bq = jnp.zeros((H,), dtype=jnp.float32)
        Wk = jax.random.normal(ks[3], (H, H), dtype=jnp.float32) * sc
        bk = jnp.zeros((H,), dtype=jnp.float32)
        Wv = jax.random.normal(ks[4], (H, H), dtype=jnp.float32) * sc
        bv = jnp.zeros((H,), dtype=jnp.float32)
        Wf = jax.random.normal(ks[5], (H, H), dtype=jnp.float32) * sc
        bf = jnp.zeros((H,), dtype=jnp.float32)
        return {'seq_inputs': seq_inputs, 'Wq': Wq, 'bq': bq, 'Wk': Wk, 'bk': bk, 'Wv': Wv, 'bv': bv, 'Wf': Wf, 'bf': bf, 'graph_mask': graph_mask}
    _L0_gnn_all = _L0_gnn_setup()
    _L0_gnn_in = {k: v for k, v in _L0_gnn_all.items() if k in ('Wq', 'bq', 'Wk', 'bk', 'Wv', 'bv', 'Wf', 'bf', )}
    del _L0_gnn_all

    def _L1_gnn_setup():
        import jax, jax.numpy as jnp
        import numpy as np
        ATT_HEAD = 12
        IN_DIM = 768
        OUT_DIM = IN_DIM // ATT_HEAD
        LEAKY_ALPHA = 0.2
        B, N = (8, 512)
        key = jax.random.key(seed)
        ks = jax.random.split(key, 8)
        feat_in = jax.random.normal(ks[0], (B, N, IN_DIM), dtype=jnp.float32)
        adj = jax.random.randint(ks[1], (B, N, N), 0, 2) > 0
        lim_W = float(np.sqrt(6.0 / (IN_DIM + OUT_DIM)))
        W = jax.random.uniform(ks[2], (ATT_HEAD, IN_DIM, OUT_DIM), minval=-lim_W, maxval=lim_W, dtype=jnp.float32)
        b = jnp.zeros((OUT_DIM,), dtype=jnp.float32)
        lim_w = float(np.sqrt(6.0 / (OUT_DIM + 1)))
        w_src = jax.random.uniform(ks[3], (ATT_HEAD, OUT_DIM, 1), minval=-lim_w, maxval=lim_w, dtype=jnp.float32)
        w_dst = jax.random.uniform(ks[4], (ATT_HEAD, OUT_DIM, 1), minval=-lim_w, maxval=lim_w, dtype=jnp.float32)
        std_H = float(np.sqrt(2.0 / (IN_DIM + IN_DIM)))
        H_w = jax.random.normal(ks[5], (IN_DIM, IN_DIM), dtype=jnp.float32) * std_H
        H_b = jax.random.normal(ks[6], (IN_DIM,), dtype=jnp.float32) * 0.01
        return {'feat_in': feat_in, 'adj': adj, 'W': W, 'b': b, 'w_src': w_src, 'w_dst': w_dst, 'H_w': H_w, 'H_b': H_b}
    _L1_gnn_all = _L1_gnn_setup()
    _L1_gnn_in = {k: v for k, v in _L1_gnn_all.items() if k in ('W', 'b', 'w_src', 'w_dst', 'H_w', 'H_b', )}
    del _L1_gnn_all

    return {
        "x": x,
        "adj": adj,
        "L0_gnn_Wq": _L0_gnn_in["Wq"],
        "L0_gnn_bq": _L0_gnn_in["bq"],
        "L0_gnn_Wk": _L0_gnn_in["Wk"],
        "L0_gnn_bk": _L0_gnn_in["bk"],
        "L0_gnn_Wv": _L0_gnn_in["Wv"],
        "L0_gnn_bv": _L0_gnn_in["bv"],
        "L0_gnn_Wf": _L0_gnn_in["Wf"],
        "L0_gnn_bf": _L0_gnn_in["bf"],
        "L1_gnn_W": _L1_gnn_in["W"],
        "L1_gnn_b": _L1_gnn_in["b"],
        "L1_gnn_w_src": _L1_gnn_in["w_src"],
        "L1_gnn_w_dst": _L1_gnn_in["w_dst"],
        "L1_gnn_H_w": _L1_gnn_in["H_w"],
        "L1_gnn_H_b": _L1_gnn_in["H_b"],
    }

def reference(x, adj, L0_gnn_Wq, L0_gnn_bq, L0_gnn_Wk, L0_gnn_bk, L0_gnn_Wv, L0_gnn_bv, L0_gnn_Wf, L0_gnn_bf, L1_gnn_W, L1_gnn_b, L1_gnn_w_src, L1_gnn_w_dst, L1_gnn_H_w, L1_gnn_H_b):
    import jax
    import jax.numpy as jnp
    def _L0_gnn_ref(seq_inputs, Wq, bq, Wk, bk, Wv, bv, Wf, bf, graph_mask):
        import jax, jax.numpy as jnp
        import numpy as np
        B, S, H = (4, 2048, 768)
        NUM_HEADS = 6
        HEAD_SIZE = H // NUM_HEADS
        NEG = -9000000000000000.0

        def _heads(x):
            b, s, _ = x.shape
            return x.reshape(b, s, NUM_HEADS, HEAD_SIZE).transpose(0, 2, 1, 3)
        q = _heads(seq_inputs @ Wq + bq)
        k = _heads(seq_inputs @ Wk + bk)
        v = _heads(seq_inputs @ Wv + bv)
        scores = jnp.einsum('bhqd,bhkd->bhqk', q, k) / np.sqrt(HEAD_SIZE)
        bias = jnp.where(graph_mask, 0.0, NEG)[:, None]
        probs = jax.nn.softmax(scores + bias, axis=-1)
        ctx = jnp.einsum('bhqk,bhkd->bhqd', probs, v)
        ctx = ctx.transpose(0, 2, 1, 3).reshape(seq_inputs.shape[0], seq_inputs.shape[1], H)
        return ctx @ Wf + bf

    def _L1_gnn_ref(feat_in, adj, W, b, w_src, w_dst, H_w, H_b):
        import jax, jax.numpy as jnp
        import numpy as np
        ATT_HEAD = 12
        IN_DIM = 768
        OUT_DIM = IN_DIM // ATT_HEAD
        LEAKY_ALPHA = 0.2
        B, N = (8, 512)
        h = jnp.einsum('bnd,ade->bane', feat_in, W)
        th = jnp.tanh(h)
        attn_src = jnp.einsum('bane,aeo->bano', th, w_src)
        attn_dst = jnp.einsum('bane,aeo->bano', th, w_dst)
        attn = attn_src + jnp.swapaxes(attn_dst, 2, 3)
        attn = jnp.where(attn >= 0, attn, LEAKY_ALPHA * attn)
        mask = ~adj[:, None, :, :]
        attn = jnp.where(mask, jnp.float32(-999.0), attn)
        attn = jax.nn.softmax(attn, axis=-1)
        feat_out = jnp.einsum('banm,bame->bane', attn, h) + b
        feat_out = jnp.swapaxes(feat_out, 1, 2).reshape(feat_in.shape[0], feat_in.shape[1], -1)
        feat_out = jax.nn.elu(feat_out)
        gate = jax.nn.sigmoid(feat_in @ H_w.T + H_b)
        return gate * feat_out + (1.0 - gate) * feat_in

    h = jnp.maximum(_layernorm(x, axis=-1), 0.0)
    x = x + _L0_gnn_ref(h, L0_gnn_Wq, L0_gnn_bq, L0_gnn_Wk, L0_gnn_bk, L0_gnn_Wv, L0_gnn_bv, L0_gnn_Wf, L0_gnn_bf, adj)
    h = jnp.maximum(_layernorm(x, axis=-1), 0.0)
    x = x + _L1_gnn_ref(h, adj, L1_gnn_W, L1_gnn_b, L1_gnn_w_src, L1_gnn_w_dst, L1_gnn_H_w, L1_gnn_H_b)
    return x


_drawn_inputs = setup_inputs


def setup_inputs(seed=0):
    import zlib

    import numpy as np

    out = dict(_drawn_inputs(seed))
    spreads = {'L0_gnn_bq': (0.0, 0.735),
     'L0_gnn_bk': (0.0, 2.0),
     'L0_gnn_bv': (0.0, 0.1),
     'L0_gnn_bf': (0.0, 0.1),
     'L1_gnn_b': (0.0, 0.1)}
    factors = {'L1_gnn_w_src': 10.908, 'L1_gnn_H_b': 38.737}
    for name, (base, spread) in spreads.items():
        noise = np.random.default_rng([zlib.crc32(name.encode()), seed]).standard_normal(out[name].shape)
        drawn = base * np.exp(spread * noise) if base else spread * noise
        out[name] = jnp.asarray(drawn.astype(out[name].dtype))
    for name, factor in factors.items():
        out[name] = (out[name] * factor).astype(out[name].dtype)
    return out
```

```python
from contextlib import ExitStack

import concourse.bass as bass
import numpy as np
from concourse import mybir


F32 = mybir.dt.float32
F16 = mybir.dt.float16
U32 = mybir.dt.uint32
U8 = mybir.dt.uint8
ALU = mybir.AluOpType
ACT = mybir.ActivationFunctionType
AX_X = mybir.AxisListType.X
AX_XY = mybir.AxisListType.XY
MAX_OVER_PARTITIONS = bass.bass_isa.ReduceOp.max

P = 128
T = 2
EPS = 1e-5
NEG_L0 = 9.0e15
NEG_L1 = -999.0
ALPHA = 0.2
DMA = 16

HN = 1024.0
W_TOP = 2.0 ** 13
HV = 2.0 ** -19
V_TOP = 2.0 ** 14
EXPONENT = 0x7F800000
TINY = 2.0 ** -100

WQ, WK, WV, WF, WL, WG = range(6)
BY_LARGEST = (WV, WL)


def after(eng, sem, count):
    if not isinstance(count, int) or count > 0:
        eng.wait_ge(sem, count)


def after_alone(eng, passed, sem, count):
    if isinstance(count, int):
        return after(eng, sem, count)
    count = eng.snap(count)
    eng.wait_ge(passed, 1)
    eng.wait_ge(sem, count)


def build_two_layer_gnn(nc, x, adj, wq, bq, wk, bk, wv, bv, wf, bf, wl, b1, w_src, w_dst, wg, bg, out):
    G, N, C = x.shape
    KT = C // P
    H0, H1 = C // 128, w_src.shape[0]
    E1 = C // H1
    GROUPS = G * N // (P * T)
    INV_SQRT_D = 1.0 / float(np.sqrt(128.0))
    assert 2 * N == P and KT == H0 and E1 == N

    x_g = x.rearrange("(g t b) n c -> g (b n) t c", t=T, b=2)
    out_g = out.rearrange("(g t b) n c -> g (b n) t c", t=T, b=2)
    adj_g = adj.rearrange("(g t b) n m -> g (b n) t m", t=T, b=2)

    with ExitStack() as ctx:
        def sb(name, shape, dt=F32):
            return ctx.enter_context(nc.sbuf_tensor(name, shape, dt))

        def sem(name):
            return ctx.enter_context(nc.semaphore(name))

        pair_att = [ctx.enter_context(nc.psum_tensor(f"pair_att{t}", [P, 1024], F32)) for t in range(2)]
        pair_prj = [ctx.enter_context(nc.psum_tensor(f"pair_prj{t}", [P, 1024], F32)) for t in range(2)]

        w_hi = sb("w_hi", [P, 6, KT, C], F16)
        w_lo = sb("w_lo", [P, 6, KT, C], F16)
        bf_row = sb("bf_row", [P, C])
        bv_row = sb("bv_row", [P, C])
        bg_row = sb("bg_row", [P, C])
        src_row = sb("src_row", [P, C])
        dst_row = sb("dst_row", [P, C])
        b1_row = sb("b1_row", [P, E1])
        bq_col = sb("bq_col", [P, KT])
        bk_col = sb("bk_col", [P, KT])
        ident = sb("ident", [P, P])
        same_graph = sb("same_graph", [P, P])
        node_eye = sb("node_eye", [P, N])
        neg_l1 = sb("neg_l1", [P, 1])
        zero = sb("zero", [P, 1])
        to_true = sb("to_true", [P, 1])
        minus_half = sb("minus_half", [P, T])
        w_top = sb("w_top", [P, 6, 2])
        w_all = sb("w_all", [P, 6, 2])
        w_pow = sb("w_pow", [P, 8])
        w_rec = sb("w_rec", [P, 8])
        w_scale = sb("w_scale", [P, 8])
        w_undo = sb("w_undo", [P, 8])
        v_bound = sb("v_bound", [P, 4])
        adj_u8 = sb("adj_u8", [P, T, N], U8)
        not_adj = sb("not_adj", [P, T, N], U8)
        bias0 = sb("bias0", [P, T, N])
        bn_out = [sb(f"bn_out{n}", [P, T, 2, 6]) for n in range(2)]
        mean_var = [sb(f"mean_var{n}", [P, T, 2]) for n in range(2)]
        var_eps = [sb(f"var_eps{n}", [P, T]) for n in range(2)]
        rstd = [sb(f"rstd{n}", [P, T]) for n in range(2)]
        shift = [sb(f"shift{n}", [P, T]) for n in range(2)]
        keep_rstd = sb("keep_rstd", [P, T])
        keep_shift = sb("keep_shift", [P, T])
        max0 = sb("max0", [P, T * H0])
        sum0 = sb("sum0", [P, T * H0])
        rinv0 = sb("rinv0", [P, T * H0])
        src_dst = sb("src_dst", [P, T, 2, H1])
        max1 = sb("max1", [P, T, H1])
        sum1 = sb("sum1", [P, T, H1])
        rinv1 = sb("rinv1", [P, T, H1])

        arena = sb("arena", [P, 23 * C])

        def units(first, n):
            return arena[:, first * C:(first + n) * C]

        def tiles(first):
            return units(first, T).rearrange("p (t c) -> p t c", t=T)

        def split(first, shape, **k):
            v = units(first, 2).bitcast(F16)
            return [v[:, n * 2 * C:(n + 1) * 2 * C].rearrange(shape, **k) for n in range(2)]

        h1v_hi, h1v_lo = split(0, "p (t c) -> p t c", t=T)
        gate = tiles(2)
        s1, s2, s3 = units(4, 1), units(5, 1), units(6, 1)
        pt1_hi, pt1_lo = split(7, "p (a n) -> p a n", a=H1)
        ht1_hi, ht1_lo = split(9, "p (k n) -> p k n", k=KT)
        keep = tiles(11)
        rows = tiles(13)
        x1 = tiles(15)
        ht0_hi, ht0_lo = split(17, "p (k n) -> p k n", k=KT)
        qt = units(19, 2).rearrange("p (k n) -> p k n", k=KT)
        ct_hi, ct_lo = split(19, "p (t k n) -> p t k n", t=T, k=KT)
        kt = units(21, 2).rearrange("p (k n) -> p k n", k=KT)
        pt0 = units(21, 2).rearrange("p (t h n) -> p t h n", t=T, h=H0)
        p0_place = sb("p0_place", [P, (T * H0 + 2) * N])
        p0 = p0_place[:, N:N + C].rearrange("p (h n) -> p h n", h=T * H0)
        p1_place = sb("p1_place", [P, (T * (H1 + 1) + 1) * N])
        p1 = p1_place[:, N:].rearrange("p (t a n) -> p t a n", t=T, a=H1 + 1)[:, :, 0:H1, :]
        vals = p1_place[:, 0:T * C].rearrange("p (t c) -> p t c", t=T)
        late_hi, late_lo = [w[:, WL:WG + 1].rearrange("p m k n -> p (m k n)").bitcast(F32) for w in (w_hi, w_lo)]
        staging = [s.rearrange("p (k n) -> p k n", k=KT)
                   for s in (units(0, 6), units(6, 6), late_hi, late_lo, units(0, 6), units(6, 6))]

        const_loaded = sem("const_loaded")
        columns_loaded = sem("columns_loaded")
        weight_loaded = [[sem(f"weight_loaded{m}_{half}") for half in range(2)] for m in range(6)]
        const_made = sem("const_made")
        eye_cleared = sem("eye_cleared")
        eye_made = sem("eye_made")
        weight_top = [sem(f"weight_top{m}") for m in range(6)]
        weight_all = sem("weight_all")
        scale_step = sem("scale_step")
        weight_scaled = sem("weight_scaled")
        weight_hi = sem("weight_hi")
        weight_ready = sem("weight_ready")
        rows_loaded = sem("rows_loaded")
        x1_loaded = sem("x1_loaded")
        adj_loaded = sem("adj_loaded")
        out_stored = sem("out_stored")
        bias0_made = sem("bias0_made")
        not_adj_made = sem("not_adj_made")
        bn_done = [sem(f"bn_done{n}") for n in range(2)]
        mean_done = [sem(f"mean_done{n}") for n in range(2)]
        var_ready = [sem(f"var_ready{n}") for n in range(2)]
        rstd_ready = [sem(f"rstd_ready{n}") for n in range(2)]
        shift_ready = [sem(f"shift_ready{n}") for n in range(2)]
        rows0_ready = sem("rows0_ready")
        rows1_ready = sem("rows1_ready")
        t0_psum = sem("t0_psum")
        ht0_hi_ready = sem("ht0_hi_ready")
        ht0_ready = sem("ht0_ready")
        t1_psum = sem("t1_psum")
        ht1_hi_ready = sem("ht1_hi_ready")
        ht1_ready = sem("ht1_ready")
        q_psum = sem("q_psum")
        q_ready = sem("q_ready")
        k_psum = sem("k_psum")
        k_ready = sem("k_ready")
        v_psum = sem("v_psum")
        v_ready = sem("v_ready")
        s_psum = sem("s_psum")
        s_ready = sem("s_ready")
        max0_ready = sem("max0_ready")
        shifted0 = sem("shifted0")
        exp0_ready = sem("exp0_ready")
        sum0_ready = sem("sum0_ready")
        rinv0_ready = sem("rinv0_ready")
        p0_ready = sem("p0_ready")
        pt0_cleared = sem("pt0_cleared")
        pt0_psum = sem("pt0_psum")
        pt0_ready = sem("pt0_ready")
        ct_psum = sem("ct_psum")
        ct_hi_ready = sem("ct_hi_ready")
        ct_ready = sem("ct_ready")
        f_psum = sem("f_psum")
        bf_added = sem("bf_added")
        x1_ready = sem("x1_ready")
        kept = sem("kept")
        h_psum = sem("h_psum")
        h_hi_ready = sem("h_hi_ready")
        th_ready = sem("th_ready")
        h_ready = sem("h_ready")
        src_prod = sem("src_prod")
        dst_prod = sem("dst_prod")
        src_ready = sem("src_ready")
        dst_ready = sem("dst_ready")
        dst_diag = sem("dst_diag")
        g_psum = sem("g_psum")
        g_ready = sem("g_ready")
        gate_ready = sem("gate_ready")
        d_psum = sem("d_psum")
        z_ready = sem("z_ready")
        leaky_ready = sem("leaky_ready")
        masked1 = sem("masked1")
        max1_ready = sem("max1_ready")
        shifted1 = sem("shifted1")
        exp1_ready = sem("exp1_ready")
        sum1_ready = sem("sum1_ready")
        rinv1_ready = sem("rinv1_ready")
        rinv1_scaled = sem("rinv1_scaled")
        pt1_cleared = sem("pt1_cleared")
        pt1_psum = sem("pt1_psum")
        pt1_hi_ready = sem("pt1_hi_ready")
        pt1_ready = sem("pt1_ready")
        o_psum = sem("o_psum")
        o_norm = sem("o_norm")
        o_biased = sem("o_biased")
        o_min = sem("o_min")
        h_again = sem("h_again")
        o_exp = sem("o_exp")
        elu_ready = sem("elu_ready")
        diff_ready = sem("diff_ready")
        gated = sem("gated")
        summed = sem("summed")
        y_ready = sem("y_ready")

        block = ctx.enter_context(nc.Block())

        def columns(half):
            return slice(half * (C // 2), (half + 1) * (C // 2))

        def diagonal(pair, g):
            v = pair.rearrange("p (w n) -> p w n", n=P)
            return v[N * g:N * g + N, 1 - g:7 - g, N * g:N * g + N]

        def steps(eng, one):
            def flags(i):
                return [0 <= g < GROUPS for g in (i, i - 1, i - 2, i + 1)]
            for i in (0, 1):
                one(i, *flags(i))
            with eng.Fori(2, GROUPS - 1) as i:
                one(i, True, True, True, True)
            for i in range(GROUPS - 1, GROUPS + 2):
                one(i, *flags(i))

        @block.sync
        def _(sp):
            weights = [wq, wk, wv, wf, wl, wg]

            def load_weight(m):
                w = weights[m].rearrange("(k p) n -> p k n", p=P)
                for half in range(2):
                    sp.dma_start(staging[m][:, :, columns(half)], w[:, :, columns(half)])\
                        .then_inc(weight_loaded[m][half], DMA)

            sp.dma_start(rows, x_g[0]).then_inc(rows_loaded, DMA)
            load_weight(WQ)
            for dst, src in ((bq_col, bq), (bk_col, bk)):
                sp.dma_start(dst[:], src).then_inc(columns_loaded, DMA)
            load_weight(WK)
            load_weight(WV)
            sp.dma_start(x1, x_g[0]).then_inc(x1_loaded, DMA)
            for dst, src in ((bf_row, bf), (bv_row, bv), (bg_row, bg), (b1_row, b1)):
                sp.dma_start(dst[:], src.partition_broadcast(P)).then_inc(const_loaded, DMA)
            for dst, src in ((src_row, w_src), (dst_row, w_dst)):
                sp.dma_start(dst[:], src.rearrange("a e o -> (a e o)").partition_broadcast(P)).then_inc(const_loaded, DMA)
            load_weight(WF)
            sp.wait_ge(weight_ready, 2 * (WQ + 1))
            load_weight(WL)
            sp.wait_ge(weight_ready, 2 * (WK + 1))
            load_weight(WG)

            def one(i, now, mid, last, nxt):
                j, p = i - 1, i - 2
                if now:
                    after_alone(sp, eye_made, not_adj_made, i)
                    sp.dma_start(adj_u8[:], adj_g[i]).then_inc(adj_loaded, DMA)
                if last:
                    after_alone(sp, eye_made, y_ready, 2 * p + 1)
                    sp.dma_start(out_g[p, :, 0, :], keep[:, 0, :]).then_inc(out_stored, DMA)
                if nxt:
                    after_alone(sp, eye_made, t0_psum, 2 * i + 2)
                    if mid:
                        after_alone(sp, eye_made, t1_psum, 2 * j + 2)
                    sp.dma_start(rows, x_g[i + 1]).then_inc(rows_loaded, DMA)
                if last:
                    after_alone(sp, eye_made, y_ready, 2 * p + 2)
                    sp.dma_start(out_g[p, :, 1, :], keep[:, 1, :]).then_inc(out_stored, DMA)
                if now and mid:
                    after_alone(sp, eye_made, rows1_ready, 2 * j + 2)
                    after_alone(sp, eye_made, kept, j + 1)
                    sp.dma_start(x1, x_g[i]).then_inc(x1_loaded, DMA)

            steps(sp, one)
            sp.wait_ge(out_stored, 2 * DMA * GROUPS)

        @block.tensor
        def _(pe):
            def weight(m, k, part):
                return (w_hi, w_lo)[part][:, m, k, :]

            def project_rows(m, lhs, t, pair, done):
                for lo, hi in ((0, 512), (512, C)):
                    for k in range(KT):
                        for n, (a, b) in enumerate(((0, 0), (0, 1), (1, 0))):
                            mm = nc.tensor.matmul(pair[:, lo:hi], lhs(a, k), weight(m, k, b)[:, lo:hi],
                                                  start=(k == 0 and n == 0), stop=(k == KT - 1 and n == 2))
                mm.then_inc(done, 1)

            def project_columns(m, half, pair, done):
                for c in range(3):
                    o = (3 * half + c) * P
                    for k in range(KT):
                        for n, (a, b) in enumerate(((0, 0), (0, 1), (1, 0))):
                            mm = nc.tensor.matmul(pair[:, c * 256:(c + 1) * 256], weight(m, k, a)[:, o:o + P],
                                                  (ht0_hi, ht0_lo)[b][:, k, :],
                                                  start=(k == 0 and n == 0), stop=(k == KT - 1 and n == 2))
                mm.then_inc(done, 1)

            def transpose_rows(t, done):
                for k in range(KT):
                    mm = nc.tensor.transpose(pair_prj[t][:, k * P:(k + 1) * P], rows[:, t, k * P:(k + 1) * P], ident[:])
                mm.then_inc(done, 1)

            def transpose_windows(pair, place, block, done):
                for w in range(7):
                    c = (block + w) * N
                    mm = nc.tensor.transpose(pair_att[pair][:, w * P:(w + 1) * P], place[:, c:c + 2 * N], ident[:])
                mm.then_inc(done, 1)

            def transpose_p1(t, half):
                transpose_windows(half, p1_place, t * (H1 + 1) + 6 * half, pt1_psum)

            def attend1(t):
                for a in range(H1):
                    c = slice(a * E1, (a + 1) * E1)
                    parts = ((pt1_hi, h1v_hi), (pt1_hi, h1v_lo), (pt1_lo, h1v_hi))
                    for n, (pt, hv) in enumerate(parts):
                        mm = nc.tensor.matmul(pair_att[t][:, c], pt[:, a, :], hv[:, t, c], start=(n == 0), stop=(n == 2))
                mm.then_inc(o_psum, 1)

            pe.wait_ge(eye_made, 2)
            for t in range(T):
                pe.wait_ge(rows0_ready, t + 1)
                transpose_rows(t, t0_psum)

            def one(i, now, mid, last, nxt):
                j, p = i - 1, i - 2
                first = isinstance(i, int) and i == 0
                first_mid = isinstance(i, int) and i == 1

                if now:
                    if first:
                        pe.wait_ge(weight_ready, 2 * WQ + 1)
                    pe.wait_ge(ht0_ready, 2 * i + 2)
                    after(pe, x1_ready, 2 * i - 1)
                    project_columns(WQ, 0, pair_prj[0], q_psum)
                if last:
                    pe.wait_ge(exp1_ready, 2 * p + 1)
                    transpose_p1(0, 0)
                    pe.wait_ge(z_ready, 2 * p + 2)
                    transpose_p1(0, 1)
                if now:
                    if first:
                        pe.wait_ge(weight_ready, 2 * WQ + 2)
                    after(pe, x1_ready, 2 * i)
                    project_columns(WQ, 1, pair_prj[1], q_psum)
                if last:
                    pe.wait_ge(h_ready, 2 * p + 2)
                    pe.wait_ge(pt1_ready, 4 * p + 2)
                    attend1(0)
                if now:
                    if first:
                        pe.wait_ge(weight_ready, 2 * WK + 1)
                    pe.wait_ge(q_ready, 2 * i + 1)
                    project_columns(WK, 0, pair_prj[0], k_psum)
                if last:
                    pe.wait_ge(exp1_ready, 2 * p + 2)
                    pe.wait_ge(o_norm, 2 * p + 1)
                    transpose_p1(1, 0)
                    transpose_p1(1, 1)
                if now:
                    if first:
                        pe.wait_ge(weight_ready, 2 * WK + 2)
                    pe.wait_ge(q_ready, 2 * i + 2)
                    project_columns(WK, 1, pair_prj[1], k_psum)
                if last:
                    pe.wait_ge(pt1_ready, 4 * p + 4)
                    attend1(1)

                if mid:
                    for t in range(T):
                        pe.wait_ge(rows1_ready, 2 * j + t + 1)
                        if now:
                            pe.wait_ge(k_ready, 2 * i + t + 1)
                        transpose_rows(t, t1_psum)

                if now:
                    pe.wait_ge(k_ready, 2 * i + 2)
                    for t in range(T):
                        if last and t == 0:
                            pe.wait_ge(pt1_ready, 4 * p + 3)
                        elif last:
                            pe.wait_ge(o_norm, 2 * p + 2)
                        else:
                            after(pe, ct_ready, 2 * i - 1 + t)
                        for h in range(H0):
                            mm = nc.tensor.matmul(pair_att[t][:, h * P:(h + 1) * P], qt[:, h, t * P:(t + 1) * P],
                                                  kt[:, h, t * P:(t + 1) * P], start=True, stop=True)
                        mm.then_inc(s_psum, 1)

                    if first:
                        pe.wait_ge(weight_ready, 2 * WV + 2)
                    for t in range(T):
                        if mid:
                            pe.wait_ge(ht1_ready, 2 * j + t + 1)
                        else:
                            pe.wait_ge(k_ready, 2 * i + t + 1)
                        project_rows(WV, lambda a, k: (ht0_hi, ht0_lo)[a][:, k, t * P:(t + 1) * P], t,
                                     pair_prj[t], v_psum)

                if mid:
                    if first_mid:
                        pe.wait_ge(weight_ready, 2 * WL + 2)
                    for t in range(T):
                        pe.wait_ge(ht1_ready, 2 * j + t + 1)
                        if now:
                            pe.wait_ge(v_ready, 2 * i + t + 1)
                        project_rows(WL, lambda a, k: (ht1_hi, ht1_lo)[a][:, k, t * P:(t + 1) * P], t,
                                     pair_prj[t], h_psum)

                if now:
                    pe.wait_ge(p0_ready, i + 1)
                    for t in range(T):
                        transpose_windows(t, p0_place, t * H0, pt0_psum)

                if nxt:
                    for t in range(T):
                        pe.wait_ge(rows0_ready, 2 * i + t + 3)
                        if mid:
                            pe.wait_ge(h_ready, 2 * j + t + 1)
                        else:
                            pe.wait_ge(v_ready, 2 * i + t + 1)
                        transpose_rows(t, t0_psum)

                if now:
                    pe.wait_ge(v_ready, 2 * i + 2)
                    for t in range(T):
                        pe.wait_ge(pt0_ready, 2 * i + t + 1)
                        for h in range(H0):
                            mm = nc.tensor.matmul(pair_att[t][:, h * P:(h + 1) * P], vals[:, t, h * P:(h + 1) * P],
                                                  pt0[:, t, h, :], start=True, stop=True)
                        mm.then_inc(ct_psum, 1)

                if mid:
                    if first_mid:
                        pe.wait_ge(weight_ready, 2 * WG + 2)
                    for t in range(T):
                        if nxt:
                            pe.wait_ge(ht0_ready, 2 * i + t + 3)
                        else:
                            pe.wait_ge(h_ready, 2 * j + t + 1)
                        project_rows(WG, lambda a, k: (ht1_hi, ht1_lo)[a][:, k, t * P:(t + 1) * P], t,
                                     pair_prj[t], g_psum)

                    for t in range(T):
                        pe.wait_ge(dst_diag, 2 * j + t + 1)
                        if now:
                            pe.wait_ge(ct_ready, 2 * i + t + 1)
                        elif last and t == 0:
                            pe.wait_ge(pt1_ready, 4 * p + 3)
                        elif last:
                            pe.wait_ge(o_norm, 2 * p + 2)
                        for lo, hi in ((0, 512), (512, C)):
                            mm = nc.tensor.matmul(pair_att[t][:, lo:hi], same_graph[:], (s2, s3)[t][:, lo:hi],
                                                  start=True, stop=True)
                        mm.then_inc(d_psum, 1)

                if now:
                    if first:
                        pe.wait_ge(weight_ready, 2 * WF + 2)
                    for t in range(T):
                        pe.wait_ge(ct_ready, 2 * i + t + 1)
                        if mid:
                            pe.wait_ge(g_ready, 2 * j + t + 1)
                        else:
                            pe.wait_ge(ht0_ready, 2 * i + t + 3)
                        project_rows(WF, lambda a, k: (ct_hi, ct_lo)[a][:, t, k, :], t, pair_prj[t], f_psum)

            steps(pe, one)

        @block.vector
        def _(dve):
            made = [0]

            def scale(ins):
                made[0] += 1
                ins.then_inc(scale_step, 1)
                dve.wait_ge(scale_step, made[0])

            def col(tensor, n):
                return tensor[:, n:n + 1]

            def power_of_two(dst, src):
                scale(nc.vector.tensor_scalar(dst.bitcast(U32), src.bitcast(U32), EXPONENT, None, ALU.bitwise_and))
                scale(nc.vector.tensor_scalar(dst, dst, TINY, None, ALU.max))

            def largest(m, half):
                dve.wait_ge(weight_loaded[m][half], DMA)
                nc.vector.tensor_reduce(w_top[:, m, half:half + 1], staging[m][:, :, columns(half)], AX_XY, ALU.max,
                                        apply_absolute_value=True).then_inc(weight_top[m], 1)

            def scale_weight(m):
                dve.wait_ge(weight_all, m + 1)
                scale(nc.vector.tensor_tensor(col(w_pow, m), w_all[:, m, 0:1], w_all[:, m, 1:2],
                                              ALU.max if m in BY_LARGEST else ALU.add))
                power_of_two(col(w_pow, m), col(w_pow, m))
                scale(nc.vector.reciprocal(col(w_rec, m), col(w_pow, m)))
                nc.vector.tensor_scalar(col(w_scale, m), col(w_rec, m), W_TOP, None, ALU.mult).then_inc(weight_scaled, 1)
                undo = 1.0 / W_TOP if m == WF else 1.0 / (W_TOP * HN)
                scale(nc.vector.tensor_scalar(col(w_undo, m), col(w_pow, m), undo, None, ALU.mult))
                if m == WV:
                    dve.wait_ge(const_loaded, 6 * DMA)
                    scale(nc.vector.tensor_reduce(col(w_pow, 6), bv_row[:], AX_X, ALU.max, apply_absolute_value=True))
                    power_of_two(col(w_pow, 6), col(w_pow, 6))
                    scale(nc.vector.tensor_scalar(col(v_bound, 0), col(w_pow, 6), 2.0, None, ALU.mult))
                    scale(nc.vector.scalar_tensor_tensor(col(v_bound, 0), col(w_pow, WV), 2048.0, col(v_bound, 0),
                                                         ALU.mult, ALU.add))
                    power_of_two(col(v_bound, 1), col(v_bound, 0))
                    scale(nc.vector.reciprocal(col(v_bound, 2), col(v_bound, 1)))
                    scale(nc.vector.tensor_scalar(col(v_bound, 2), col(v_bound, 2), V_TOP, None, ALU.mult))
                    scale(nc.vector.tensor_scalar(bv_row[:], bv_row[:], col(v_bound, 2), None, ALU.mult))
                    scale(nc.vector.tensor_tensor(col(w_undo, WV), col(w_undo, WV), col(v_bound, 2), ALU.mult))
                if m == WF:
                    scale(nc.vector.tensor_scalar(col(v_bound, 3), col(v_bound, 1), 1.0 / V_TOP, None, ALU.mult))
                    scale(nc.vector.tensor_tensor(col(w_undo, WF), col(w_undo, WF), col(v_bound, 3), ALU.mult))
                if m == WL:
                    scale(nc.vector.tensor_scalar(col(w_undo, 7), col(w_undo, WL), 1.0 / HV, None, ALU.mult))

            def low_weight(m, half):
                dve.wait_ge(weight_hi, 2 * m + half + 1)
                nc.vector.scalar_tensor_tensor(w_lo[:, m, :, columns(half)], staging[m][:, :, columns(half)],
                                               col(w_scale, m), w_hi[:, m, :, columns(half)],
                                               ALU.mult, ALU.subtract).then_inc(weight_ready, 1)

            def statistics(n, src, g):
                for t in range(T):
                    for c in range(2):
                        bn = nc.vector.bn_stats(bn_out[n][:, t, c, :], src[:, t, c * (C // 2):(c + 1) * (C // 2)])
                bn.then_inc(bn_done[n], 1)
                after_alone(dve, eye_made, bn_done[n], g + 1)
                for t in range(T):
                    ag = nc.vector.bn_aggr(mean_var[n][:, t, :], bn_out[n][:, t].rearrange("p c s -> p (c s)"))
                ag.then_inc(mean_done[n], 1)
                dve.wait_ge(mean_done[n], g + 1)
                nc.vector.tensor_scalar(var_eps[n][:], mean_var[n][:, :, 1], EPS, 1.0 / (HN * HN), ALU.add, ALU.mult)\
                    .then_inc(var_ready[n], 1)
                dve.wait_ge(rstd_ready[n], g + 1)
                nc.vector.scalar_tensor_tensor(shift[n][:], mean_var[n][:, :, 0], -1.0, rstd[n][:],
                                               ALU.mult, ALU.mult).then_inc(shift_ready[n], 1)

            def low_part_transposed(t, g, hi_t, lo_t, hi_ready, ready):
                dve.wait_ge(hi_ready, 2 * g + t + 1)
                nc.vector.tensor_tensor(lo_t[:, :, t * P:(t + 1) * P],
                                        pair_prj[t][:, 0:C].rearrange("p (k n) -> p k n", k=KT),
                                        hi_t[:, :, t * P:(t + 1) * P], ALU.subtract).then_inc(ready, 1)

            def biased_columns(half, pair, dst, bias, m, ready):
                nc.vector.scalar_tensor_tensor(
                    dst[:, 3 * half:3 * half + 3, :], pair[:, 0:C].rearrange("p (c n) -> p c n", c=3), col(w_undo, m),
                    bias[:, 3 * half:3 * half + 3].unsqueeze(2).broadcast_to([P, 3, 2 * P]),
                    ALU.mult, ALU.add).then_inc(ready, 1)

            def pt1_low(t, half, p):
                dve.wait_ge(pt1_hi_ready, 4 * p + 2 * t + half + 1)
                heads = slice(6 * half, 6 * half + 6)
                for g in range(2):
                    r = slice(N * g, N * g + N)
                    lo = nc.vector.tensor_tensor(
                        pt1_lo[r, heads, r], diagonal(pair_att[half][:], g), pt1_hi[r, heads, r], ALU.subtract)
                lo.then_inc(pt1_ready, 1)

            def heads1(ap):
                return ap.rearrange("p (a n) -> p a n", a=H1)

            def output_first(t, p):
                dve.wait_ge(o_psum, 2 * p + t + 1)
                nc.vector.tensor_tensor(heads1(s1), heads1(pair_att[t][:, 0:C]),
                                        rinv1[:, t, :].unsqueeze(2).broadcast_to([P, H1, E1]), ALU.mult)\
                    .then_inc(o_norm, 1)

            def output_min(t, p):
                dve.wait_ge(o_biased, 2 * p + t + 1)
                nc.vector.tensor_scalar(s2, s1, 0.0, None, ALU.min).then_inc(o_min, 1)

            def output_last(t, p):
                n = 2 * p + t + 1
                dve.wait_ge(o_exp, n)
                nc.vector.scalar_tensor_tensor(s1, s2, -1.0, s1, ALU.add, ALU.max).then_inc(elu_ready, 1)
                dve.wait_ge(elu_ready, n)
                dve.wait_ge(h_again, n)
                nc.vector.tensor_tensor(s2, s1, s3, ALU.subtract).then_inc(diff_ready, 1)
                dve.wait_ge(diff_ready, n)
                dve.wait_ge(gate_ready, n)
                nc.vector.scalar_tensor_tensor(s2, gate[:, t, :], 1.0, s2, ALU.add, ALU.mult).then_inc(gated, 1)
                dve.wait_ge(gated, n)
                nc.vector.scalar_tensor_tensor(keep[:, t, :], s2, 0.5, keep[:, t, :], ALU.mult, ALU.add)\
                    .then_inc(summed, 1)

            dve.wait_ge(eye_cleared, 4)
            dve.wait_ge(rows_loaded, DMA)
            statistics(0, rows, 0)
            scale_weight(WQ)
            low_weight(WQ, 0)
            for t in range(T):
                low_part_transposed(t, 0, ht0_hi, ht0_lo, ht0_hi_ready, ht0_ready)
            low_weight(WQ, 1)
            largest(WV, 0)
            scale_weight(WK)
            largest(WV, 1)
            low_weight(WK, 0)
            dve.wait_ge(columns_loaded, 2 * DMA)

            def one(i, now, mid, last, nxt):
                j, p = i - 1, i - 2
                first = isinstance(i, int) and i == 0
                if mid:
                    dve.wait_ge(x1_ready, 2 * j + 2)
                    statistics(1, x1, j)
                if now:
                    dve.wait_ge(q_psum, 2 * i + 1)
                    biased_columns(0, pair_prj[0], qt, bq_col, WQ, q_ready)
                if first:
                    low_weight(WK, 1)
                    scale_weight(WV)
                if last:
                    pt1_low(0, 0, p)
                    pt1_low(0, 1, p)
                if now:
                    dve.wait_ge(q_psum, 2 * i + 2)
                    biased_columns(1, pair_prj[1], qt, bq_col, WQ, q_ready)
                if first:
                    low_weight(WV, 0)
                if last:
                    dve.wait_ge(rinv1_scaled, 2 * p + 2)
                    output_first(0, p)
                    output_min(0, p)
                if now:
                    dve.wait_ge(k_psum, 2 * i + 1)
                    biased_columns(0, pair_prj[0], kt, bk_col, WK, k_ready)
                if first:
                    low_weight(WV, 1)
                    scale_weight(WF)
                if last:
                    output_last(0, p)
                    pt1_low(1, 0, p)
                    pt1_low(1, 1, p)
                if now:
                    dve.wait_ge(k_psum, 2 * i + 2)
                    biased_columns(1, pair_prj[1], kt, bk_col, WK, k_ready)
                if last:
                    output_first(1, p)
                if mid:
                    low_part_transposed(0, j, ht1_hi, ht1_lo, ht1_hi_ready, ht1_ready)
                if last:
                    output_min(1, p)
                if mid:
                    low_part_transposed(1, j, ht1_hi, ht1_lo, ht1_hi_ready, ht1_ready)
                if last:
                    output_last(1, p)

                if now:
                    dve.wait_ge(adj_loaded, DMA * (i + 1))
                    nc.vector.tensor_scalar(bias0[:], adj_u8[:], -1.0, NEG_L0, ALU.add, ALU.mult).then_inc(bias0_made, 1)
                    dve.wait_ge(bias0_made, i + 1)
                    for t in range(T):
                        dve.wait_ge(s_psum, 2 * i + t + 1)
                        for g in range(2):
                            r = slice(N * g, N * g + N)
                            sc = nc.vector.scalar_tensor_tensor(
                                p0[r, t * H0:(t + 1) * H0, :],
                                pair_att[t][r, 0:C].rearrange("p (h n) -> p h n", h=H0)[:, :, r], INV_SQRT_D,
                                bias0[r, t, :].unsqueeze(1).broadcast_to([N, H0, N]), ALU.mult, ALU.add)
                        sc.then_inc(s_ready, 1)
                    wide = [P, T * H0, N]
                    dve.wait_ge(s_ready, 2 * i + 2)
                    nc.vector.tensor_reduce(max0[:], p0, AX_X, ALU.max).then_inc(max0_ready, 1)
                    dve.wait_ge(max0_ready, i + 1)
                    nc.vector.tensor_tensor(p0, p0, max0[:].unsqueeze(2).broadcast_to(wide), ALU.subtract)\
                        .then_inc(shifted0, 1)

                    if first:
                        low_weight(WF, 0)
                    dve.wait_ge(v_psum, 2 * i + 1)
                    nc.vector.scalar_tensor_tensor(vals[:, 0, :], pair_prj[0][:, 0:C], col(w_undo, WV), bv_row[:],
                                                   ALU.mult, ALU.add).then_inc(v_ready, 1)
                    dve.wait_ge(exp0_ready, i + 1)
                    nc.vector.tensor_reduce(sum0[:], p0, AX_X, ALU.add).then_inc(sum0_ready, 1)
                    dve.wait_ge(sum0_ready, i + 1)
                    nc.vector.reciprocal(rinv0[:], sum0[:]).then_inc(rinv0_ready, 1)
                    dve.wait_ge(rinv0_ready, i + 1)
                    nc.vector.tensor_tensor(p0, p0, rinv0[:].unsqueeze(2).broadcast_to(wide), ALU.mult)\
                        .then_inc(p0_ready, 1)
                    if first:
                        low_weight(WF, 1)
                    dve.wait_ge(v_psum, 2 * i + 2)
                    nc.vector.scalar_tensor_tensor(vals[:, 1, :], pair_prj[1][:, 0:C], col(w_undo, WV), bv_row[:],
                                                   ALU.mult, ALU.add).then_inc(v_ready, 1)
                if nxt:
                    dve.wait_ge(rows_loaded, DMA * (i + 2))
                    statistics(0, rows, i + 1)

                def h_low(t):
                    dve.wait_ge(th_ready, 2 * j + t + 1)
                    nc.vector.scalar_tensor_tensor(h1v_lo[:, t, :], pair_prj[t][:, 0:C], HV, h1v_hi[:, t, :],
                                                   ALU.mult, ALU.subtract).then_inc(h_ready, 1)

                def source_and_target(t):
                    dve.wait_ge(src_prod, 2 * j + t + 1)
                    nc.vector.tensor_reduce(src_dst[:, t, 0, :], heads1(s2), AX_X, ALU.add).then_inc(src_ready, 1)
                    dve.wait_ge(dst_prod, 2 * j + t + 1)
                    nc.vector.tensor_reduce(src_dst[:, t, 1, :], heads1(s3), AX_X, ALU.add).then_inc(dst_ready, 1)

                if mid:
                    h_low(0)
                    source_and_target(0)
                    h_low(1)
                if nxt:
                    for t in range(T):
                        low_part_transposed(t, i + 1, ht0_hi, ht0_lo, ht0_hi_ready, ht0_ready)
                if now:
                    for t in range(T):
                        dve.wait_ge(ct_hi_ready, 2 * i + t + 1)
                        nc.vector.tensor_tensor(ct_lo[:, t].rearrange("p k n -> p (k n)"), pair_att[t][:, 0:C],
                                                ct_hi[:, t].rearrange("p k n -> p (k n)"), ALU.subtract)\
                            .then_inc(ct_ready, 1)
                if first:
                    largest(WL, 0)
                    largest(WL, 1)

                def keep_x1(t):
                    dve.wait_ge(bf_added, 2 * i + t + 1)
                    dve.wait_ge(f_psum, 2 * i + t + 1)
                    nc.vector.scalar_tensor_tensor(x1[:, t, :], pair_prj[t][:, 0:C], col(w_undo, WF), x1[:, t, :],
                                                   ALU.mult, ALU.add).then_inc(x1_ready, 1)

                def logits(t):
                    dve.wait_ge(d_psum, 2 * j + t + 1)
                    dve.wait_ge(src_ready, 2 * j + t + 1)
                    nc.vector.tensor_tensor(p1[:, t], heads1(pair_att[t][:, 0:C]),
                                            src_dst[:, t, 0, :].unsqueeze(2).broadcast_to([P, H1, N]), ALU.add)\
                        .then_inc(z_ready, 1)

                def mask_and_shift(t):
                    n = 2 * j + t + 1
                    dve.wait_ge(z_ready, n)
                    nc.vector.scalar_tensor_tensor(p1[:, t], p1[:, t], ALPHA, p1[:, t], ALU.mult, ALU.max)\
                        .then_inc(leaky_ready, 1)
                    after_alone(dve, eye_made, leaky_ready, n)
                    nc.vector.copy_predicated(p1[:, t], not_adj[:, t, :].unsqueeze(1).broadcast_to([P, H1, N]),
                                              neg_l1[:].unsqueeze(2).broadcast_to([P, H1, N])).then_inc(masked1, 1)
                    dve.wait_ge(masked1, n)
                    nc.vector.tensor_reduce(max1[:, t, :], p1[:, t], AX_X, ALU.max).then_inc(max1_ready, 1)
                    dve.wait_ge(max1_ready, n)
                    nc.vector.tensor_tensor(p1[:, t], p1[:, t], max1[:, t, :].unsqueeze(2).broadcast_to([P, H1, N]),
                                            ALU.subtract).then_inc(shifted1, 1)

                def sum_and_invert(t):
                    n = 2 * j + t + 1
                    dve.wait_ge(exp1_ready, n)
                    nc.vector.tensor_reduce(sum1[:, t, :], p1[:, t], AX_X, ALU.add).then_inc(sum1_ready, 1)
                    dve.wait_ge(sum1_ready, n)
                    nc.vector.reciprocal(rinv1[:, t, :], sum1[:, t, :]).then_inc(rinv1_ready, 1)
                    dve.wait_ge(rinv1_ready, n)
                    nc.vector.tensor_scalar(rinv1[:, t, :], rinv1[:, t, :], col(w_undo, 7), None, ALU.mult)\
                        .then_inc(rinv1_scaled, 1)

                if mid:
                    source_and_target(1)
                    for t in range(T):
                        dve.wait_ge(g_psum, 2 * j + t + 1)
                        nc.vector.scalar_tensor_tensor(gate[:, t, :], pair_prj[t][:, 0:C], col(w_undo, WG), bg_row[:],
                                                       ALU.mult, ALU.add).then_inc(g_ready, 1)
                    logits(0)
                    logits(1)
                    after_alone(dve, eye_made, not_adj_made, j + 1)
                    mask_and_shift(0)
                if now:
                    keep_x1(0)
                if first:
                    scale_weight(WL)
                if mid:
                    mask_and_shift(1)
                    sum_and_invert(0)
                if now:
                    keep_x1(1)
                if mid:
                    sum_and_invert(1)
                if now:
                    after(dve, masked1, 2 * j + 2)
                    nc.vector.tensor_scalar(not_adj[:], adj_u8[:], -1.0, 1.0, ALU.mult, ALU.add)\
                        .then_inc(not_adj_made, 1)
                if first:
                    scale_weight(WG)
                    for m in (WL, WG):
                        for half in range(2):
                            low_weight(m, half)

            steps(dve, one)

        @block.scalar
        def _(act):
            def magnitudes(m, half):
                act.wait_ge(weight_loaded[m][half], DMA)
                nc.scalar.activation(w_hi[:, m, :, columns(half)], staging[m][:, :, columns(half)], ACT.Abs,
                                     accum_out=w_top[:, m, half:half + 1]).then_inc(weight_top[m], 1)

            def high_weight(m, half):
                act.wait_ge(weight_scaled, m + 1)
                nc.scalar.activation(w_hi[:, m, :, columns(half)], staging[m][:, :, columns(half)], ACT.Copy,
                                     scale=w_scale[:, m:m + 1]).then_inc(weight_hi, 1)

            def normalise(n, src, ready):
                for t in range(T):
                    nc.scalar.activation(rows[:, t, :], src[:, t, :], ACT.Relu, bias=shift[n][:, t:t + 1],
                                         scale=rstd[n][:, t:t + 1]).then_inc(ready, 1)

            def high_part_transposed(t, g, psum, hi_t, hi_ready):
                act.wait_ge(psum, 2 * g + t + 1)
                nc.scalar.activation(hi_t[:, :, t * P:(t + 1) * P],
                                     pair_prj[t][:, 0:C].rearrange("p (k n) -> p k n", k=KT), ACT.Copy)\
                    .then_inc(hi_ready, 1)

            def pt1_high(t, half, p):
                act.wait_ge(pt1_psum, 4 * p + 2 * t + half + 1)
                for g in range(2):
                    r = slice(N * g, N * g + N)
                    hi = nc.scalar.activation(
                        pt1_hi[r, 6 * half:6 * half + 6, r], diagonal(pair_att[half][:], g), ACT.Copy)
                hi.then_inc(pt1_hi_ready, 1)

            def output_parts(t, p):
                after(act, y_ready, 2 * p + t)
                act.wait_ge(kept, p + 1)
                nc.scalar.activation(s3, keep[:, t, :], ACT.Relu, bias=keep_shift[:, t:t + 1],
                                     scale=keep_rstd[:, t:t + 1]).then_inc(h_again, 1)
                act.wait_ge(o_min, 2 * p + t + 1)
                nc.scalar.activation(s2, s2, ACT.Exp).then_inc(o_exp, 1)

            act.wait_ge(const_made, 6)
            magnitudes(WQ, 0)
            act.wait_ge(shift_ready[0], 1)
            normalise(0, rows, rows0_ready)
            magnitudes(WQ, 1)
            high_weight(WQ, 0)
            for t in range(T):
                high_part_transposed(t, 0, t0_psum, ht0_hi, ht0_hi_ready)
            high_weight(WQ, 1)
            for half in range(2):
                magnitudes(WK, half)
            for m in (WK, WV):
                for half in range(2):
                    high_weight(m, half)
            for half in range(2):
                magnitudes(WF, half)
            for half in range(2):
                high_weight(WF, half)

            def one(i, now, mid, last, nxt):
                j, p = i - 1, i - 2
                first = isinstance(i, int) and i == 0
                if isinstance(i, int) and i == 1:
                    act.wait_ge(weight_ready, 12)
                if isinstance(i, int) and i == 2:
                    act.wait_ge(pt1_cleared, 1)
                if mid:
                    act.wait_ge(shift_ready[1], j + 1)
                    act.wait_ge(t0_psum, 2 * i + 2 if now else 2 * GROUPS)
                    normalise(1, x1, rows1_ready)
                if last:
                    pt1_high(0, 0, p)
                    pt1_high(0, 1, p)
                    output_parts(0, p)
                    pt1_high(1, 0, p)
                    pt1_high(1, 1, p)
                if mid:
                    for t in range(T):
                        high_part_transposed(t, j, t1_psum, ht1_hi, ht1_hi_ready)
                if last:
                    output_parts(1, p)
                if now:
                    act.wait_ge(shifted0, i + 1)
                    nc.scalar.activation(p0, p0, ACT.Exp).then_inc(exp0_ready, 1)
                if now:
                    act.wait_ge(s_psum, 2 * i + 2)
                    nc.scalar.activation(units(21, 2), zero[:].broadcast_to([P, 2 * C]), ACT.Copy)\
                        .then_inc(pt0_cleared, 1)
                if nxt:
                    act.wait_ge(shift_ready[0], i + 2)
                    normalise(0, rows, rows0_ready)
                if mid:
                    for t in range(T):
                        act.wait_ge(h_psum, 2 * j + t + 1)
                        nc.scalar.activation(h1v_hi[:, t, :], pair_prj[t][:, 0:C], ACT.Copy, scale=HV)\
                            .then_inc(h_hi_ready, 1)
                        if t == 0:
                            after(act, diff_ready, 2 * p + 2)
                        else:
                            act.wait_ge(dst_prod, 2 * j + 1)
                        nc.scalar.activation(s1, pair_prj[t][:, 0:C], ACT.Tanh, scale=w_undo[:, WL:WL + 1])\
                            .then_inc(th_ready, 1)
                if now:
                    act.wait_ge(pt0_cleared, i + 1)
                    for t in range(T):
                        act.wait_ge(pt0_psum, 2 * i + t + 1)
                        for g in range(2):
                            r = slice(N * g, N * g + N)
                            pt = nc.scalar.activation(
                                pt0[r, t, :, r], diagonal(pair_att[t][:], g), ACT.Copy)
                        pt.then_inc(pt0_ready, 1)
                if nxt:
                    for t in range(T):
                        high_part_transposed(t, i + 1, t0_psum, ht0_hi, ht0_hi_ready)
                if now:
                    for t in range(T):
                        act.wait_ge(ct_psum, 2 * i + t + 1)
                        nc.scalar.activation(ct_hi[:, t].rearrange("p k n -> p (k n)"), pair_att[t][:, 0:C], ACT.Copy)\
                            .then_inc(ct_hi_ready, 1)
                if first:
                    act.wait_ge(weight_ready, 2 * (WV + 1))
                    for half in range(2):
                        magnitudes(WG, half)
                if mid:
                    for t in range(T):
                        act.wait_ge(g_ready, 2 * j + t + 1)
                        nc.scalar.activation(gate[:, t, :], gate[:, t, :], ACT.Tanh, scale=0.5).then_inc(gate_ready, 1)
                    for t in range(T):
                        act.wait_ge(shifted1, 2 * j + t + 1)
                        nc.scalar.activation(p1[:, t], p1[:, t], ACT.Exp).then_inc(exp1_ready, 1)
                if first:
                    for m in (WL, WG):
                        for half in range(2):
                            high_weight(m, half)

            steps(act, one)

        @block.gpsimd
        def _(pool):
            nc.gpsimd.memset(ident[:], 0.0).then_inc(eye_cleared, 1)
            pool.wait_ge(eye_cleared, 1)
            nc.gpsimd.affine_select(out=ident[:], in_=ident[:], compare_op=ALU.not_equal, fill=1.0, base=0,
                                    pattern=[[-1, P]], channel_multiplier=1).then_inc(eye_made, 1)
            nc.gpsimd.memset(same_graph[:], 0.0).then_inc(eye_cleared, 1)
            nc.gpsimd.memset(neg_l1[:], NEG_L1).then_inc(const_made, 1)
            nc.gpsimd.memset(minus_half[:], -0.5).then_inc(const_made, 1)
            nc.gpsimd.memset(zero[:], 0.0).then_inc(const_made, 1)
            nc.gpsimd.memset(to_true[:], 1.0 / HN).then_inc(const_made, 1)
            pool.wait_ge(eye_cleared, 2)
            for g in range(2):
                pool.wait_ge(const_made, 4 + g)
                nc.gpsimd.memset(same_graph[N * g:N * g + N, N * g:N * g + N], 1.0).then_inc(const_made, 1)
            pool.wait_ge(const_made, 6)
            nc.gpsimd.memset(p0_place[:], 0.0).then_inc(eye_cleared, 1)
            nc.gpsimd.memset(p1_place[:], 0.0).then_inc(eye_cleared, 1)
            pool.wait_ge(eye_made, 1)
            nc.gpsimd.tensor_tensor(node_eye[:], ident[:, 0:N], ident[:, N:P], ALU.add).then_inc(eye_made, 1)
            pool.wait_ge(const_made, 6)

            def top_weight(m):
                pool.wait_ge(weight_top[m], 2)
                nc.gpsimd.partition_all_reduce(w_all[:, m], w_top[:, m], P, MAX_OVER_PARTITIONS)\
                    .then_inc(weight_all, 1)

            def power(n, g):
                pool.wait_ge(var_ready[n], g + 1)
                nc.gpsimd.tensor_tensor(rstd[n][:], var_eps[n][:], minus_half[:], ALU.pow).then_inc(rstd_ready[n], 1)

            power(0, 0)
            for m in (WQ, WK, WV, WF):
                top_weight(m)
            pool.wait_ge(eye_made, 2)
            pool.wait_ge(const_loaded, 6 * DMA)

            def one(i, now, mid, last, nxt):
                j, p = i - 1, i - 2
                first = isinstance(i, int) and i == 0
                if isinstance(i, int) and i == 1:
                    pool.wait_ge(weight_ready, 12)
                    nc.gpsimd.memset(units(7, 2), 0.0).then_inc(pt1_cleared, 1)
                if mid:
                    power(1, j)
                if last:
                    for t in range(T):
                        pool.wait_ge(o_norm, 2 * p + t + 1)
                        o = s1.rearrange("p (a n) -> p a n", a=H1)
                        nc.gpsimd.tensor_tensor(o, o, b1_row[:].unsqueeze(1).broadcast_to([P, H1, E1]), ALU.add)\
                            .then_inc(o_biased, 1)
                        pool.wait_ge(summed, 2 * p + t + 1)
                        nc.gpsimd.tensor_tensor(keep[:, t, :], keep[:, t, :], s3, ALU.add).then_inc(y_ready, 1)
                if mid:
                    after(pool, out_stored, 2 * DMA * j)
                    after(pool, rows1_ready, 2 * j + 2)
                    both = to_true[:].broadcast_to([P, T])
                    nc.gpsimd.tensor_tensor(keep_rstd[:], rstd[1][:], both, ALU.mult)
                    nc.gpsimd.tensor_tensor(keep_shift[:], shift[1][:], both, ALU.mult)
                    nc.gpsimd.tensor_copy(keep, x1).then_inc(kept, 1)
                if nxt:
                    power(0, i + 1)
                if mid:
                    for t in range(T):
                        pool.wait_ge(th_ready, 2 * j + t + 1)
                        if t == 0:
                            after(pool, summed, 2 * p + 2)
                        else:
                            pool.wait_ge(dst_ready, 2 * j + 1)
                        nc.gpsimd.tensor_tensor(s2, s1, src_row[:], ALU.mult).then_inc(src_prod, 1)
                        nc.gpsimd.tensor_tensor(s3, s1, dst_row[:], ALU.mult).then_inc(dst_prod, 1)
                if now:
                    pool.wait_ge(x1_loaded, DMA * (i + 1))
                    for t in range(T):
                        nc.gpsimd.tensor_tensor(x1[:, t, :], x1[:, t, :], bf_row[:], ALU.add).then_inc(bf_added, 1)
                if mid:
                    for t in range(T):
                        pool.wait_ge(dst_ready, 2 * j + 2)
                        nc.gpsimd.tensor_tensor(
                            (s2, s3)[t].rearrange("p (a n) -> p a n", a=H1),
                            node_eye[:].unsqueeze(1).broadcast_to([P, H1, N]),
                            src_dst[:, t, 1, :].unsqueeze(2).broadcast_to([P, H1, N]), ALU.mult).then_inc(dst_diag, 1)
                if first:
                    top_weight(WL)
                    top_weight(WG)

            steps(pool, one)


_INS = ['x', 'adj', 'L0_gnn_Wq', 'L0_gnn_bq', 'L0_gnn_Wk', 'L0_gnn_bk', 'L0_gnn_Wv', 'L0_gnn_bv', 'L0_gnn_Wf',
        'L0_gnn_bf', 'L1_gnn_W', 'L1_gnn_b', 'L1_gnn_w_src', 'L1_gnn_w_dst', 'L1_gnn_H_w', 'L1_gnn_H_b']


def kernel(**inputs):
    import concourse.bacc as bacc
    from concourse.bass_utils import run_bass_kernel_spmd

    arrays = {name: np.ascontiguousarray(inputs[name]) for name in _INS}

    for name in ('L0_gnn_bq', 'L0_gnn_bk'):
        arrays[name] = np.ascontiguousarray(arrays[name].reshape(-1, P).T)
    heads, features, width = arrays['L1_gnn_W'].shape
    arrays['L1_gnn_W'] = np.ascontiguousarray(arrays['L1_gnn_W'].transpose(1, 0, 2).reshape(features, heads * width))
    arrays['L1_gnn_H_w'] = np.ascontiguousarray(arrays['L1_gnn_H_w'].T)

    nc = bacc.Bacc("TRN2", target_bir_lowering=False, num_devices=1)
    args = [nc.dram_tensor(f"in_{n}", arrays[n].shape, mybir.dt.from_np(arrays[n].dtype), kind="ExternalInput").ap()
            for n in _INS]
    out = nc.dram_tensor("out_0", arrays['x'].shape, F32, kind="ExternalOutput").ap()
    build_two_layer_gnn(nc, *args, out)
    r = run_bass_kernel_spmd(nc, [{f"in_{n}": arrays[n] for n in _INS}], core_ids=[0])
    return r.results[0]["out_0"]
```

```python
from contextlib import ExitStack

import concourse.bass as bass
import numpy as np
from concourse import mybir


F32 = mybir.dt.float32
F16 = mybir.dt.float16
BF16 = mybir.dt.bfloat16
U32 = mybir.dt.uint32
U8 = mybir.dt.uint8
ALU = mybir.AluOpType
ACT = mybir.ActivationFunctionType
AX_X = mybir.AxisListType.X
AX_XY = mybir.AxisListType.XY
MAX_OVER_PARTITIONS = bass.bass_isa.ReduceOp.max

P = 128
T = 2
EPS = 1e-5
NEG_L0 = 9.0e15
NEG_L1 = -999.0
ALPHA = 0.2
DMA = 16

HN = 1024.0
W_TOP = 2.0 ** 13
HV = 2.0 ** -19
V_TOP = 2.0 ** 14
EXPONENT = 0x7F800000
TINY = 2.0 ** -100

WQ, WK, WV, WF, WL, WG = range(6)
BY_LARGEST = (WV, WL)


def after(eng, sem, count):
    if not isinstance(count, int) or count > 0:
        eng.wait_ge(sem, count)


def after_alone(eng, passed, sem, count):
    if isinstance(count, int):
        return after(eng, sem, count)
    count = eng.snap(count)
    eng.wait_ge(passed, 1)
    eng.wait_ge(sem, count)


def build_two_layer_gnn(nc, x, adj, wq, bq, wk, bk, wv, bv, wf, bf, wl, b1, w_src, w_dst, wg, bg, out):
    G, N, C = x.shape
    KT = C // P
    H0, H1 = C // 128, w_src.shape[0]
    E1 = C // H1
    PARTS1 = 3 * H1
    GROUPS = G * N // (P * T)
    INV_SQRT_D = 1.0 / float(np.sqrt(128.0))
    assert 2 * N == P and KT == H0 and E1 == N

    x_g = x.rearrange("(g t b) n c -> g (b n) t c", t=T, b=2)
    out_g = out.rearrange("(g t b) n c -> g (b n) t c", t=T, b=2)
    adj_g = adj.rearrange("(g t b) n m -> g (b n) t m", t=T, b=2)

    with ExitStack() as ctx:
        def sb(name, shape, dt=F32):
            return ctx.enter_context(nc.sbuf_tensor(name, shape, dt))

        def sem(name):
            return ctx.enter_context(nc.semaphore(name))

        pair_att = [ctx.enter_context(nc.psum_tensor(f"pair_att{t}", [P, 1024], F32)) for t in range(2)]
        pair_prj = [ctx.enter_context(nc.psum_tensor(f"pair_prj{t}", [P, 1024], F32)) for t in range(2)]

        w_hi = sb("w_hi", [P, 6, KT, C], F16)
        w_lo = sb("w_lo", [P, 6, KT, C], F16)
        bf_row = sb("bf_row", [P, C])
        bv_row = sb("bv_row", [P, C])
        bg_row = sb("bg_row", [P, C])
        src_row = sb("src_row", [P, C])
        dst_row = sb("dst_row", [P, C])
        b1_row = sb("b1_row", [P, E1])
        bq_col = sb("bq_col", [P, KT])
        bk_col = sb("bk_col", [P, KT])
        ident = sb("ident", [P, P])
        ident_bf = sb("ident_bf", [P, P], BF16)
        in_graph = sb("in_graph", [P, 2])
        node_eye = sb("node_eye", [P, N], BF16)
        of_head = sb("of_head", [P, H1])
        of_graph = sb("of_graph", [P, 2])
        logit_lhs = sb("logit_lhs", [P, T, P], BF16)
        dst_terms = sb("dst_terms", [P, T, 3 * PARTS1], BF16)
        parts = sb("parts", [P, T, 2, PARTS1], BF16)
        rest = sb("rest", [P, T, 2, H1])
        neg_l1 = sb("neg_l1", [P, 1])
        zero = sb("zero", [P, 1])
        to_true = sb("to_true", [P, 1])
        minus_half = sb("minus_half", [P, T])
        w_top = sb("w_top", [P, 6, 2])
        w_all = sb("w_all", [P, 6, 2])
        w_pow = sb("w_pow", [P, 8])
        w_rec = sb("w_rec", [P, 8])
        w_scale = sb("w_scale", [P, 8])
        w_undo = sb("w_undo", [P, 8])
        v_bound = sb("v_bound", [P, 4])
        adj_u8 = sb("adj_u8", [P, T, N], U8)
        not_adj = sb("not_adj", [P, T, N], U8)
        bias0 = sb("bias0", [P, T, N])
        bn_out = [sb(f"bn_out{n}", [P, T, 2, 6]) for n in range(2)]
        mean_var = [sb(f"mean_var{n}", [P, T, 2]) for n in range(2)]
        var_eps = [sb(f"var_eps{n}", [P, T]) for n in range(2)]
        rstd = [sb(f"rstd{n}", [P, T]) for n in range(2)]
        shift = [sb(f"shift{n}", [P, T]) for n in range(2)]
        keep_rstd = sb("keep_rstd", [P, T])
        keep_shift = sb("keep_shift", [P, T])
        max0 = sb("max0", [P, T * H0])
        sum0 = sb("sum0", [P, T * H0])
        rinv0 = sb("rinv0", [P, T * H0])
        src_dst = sb("src_dst", [P, T, 2, H1])
        max1 = sb("max1", [P, T, H1])
        sum1 = sb("sum1", [P, T, H1])
        rinv1 = sb("rinv1", [P, T, H1])

        arena = sb("arena", [P, 23 * C])

        def units(first, n):
            return arena[:, first * C:(first + n) * C]

        def tiles(first):
            return units(first, T).rearrange("p (t c) -> p t c", t=T)

        def split(first, shape, **k):
            v = units(first, 2).bitcast(F16)
            return [v[:, n * 2 * C:(n + 1) * 2 * C].rearrange(shape, **k) for n in range(2)]

        h1v_hi, h1v_lo = split(0, "p (t c) -> p t c", t=T)
        gate = tiles(2)
        s1, s2, s3 = units(4, 1), units(5, 1), units(6, 1)
        pt1_hi, pt1_lo = split(7, "p (a n) -> p a n", a=H1)
        ht1_hi, ht1_lo = split(9, "p (k n) -> p k n", k=KT)
        keep = tiles(11)
        rows = tiles(13)
        x1 = tiles(15)
        ht0_hi, ht0_lo = split(17, "p (k n) -> p k n", k=KT)
        qt = units(19, 2).rearrange("p (k n) -> p k n", k=KT)
        ct_hi, ct_lo = split(19, "p (t k n) -> p t k n", t=T, k=KT)
        kt = units(21, 2).rearrange("p (k n) -> p k n", k=KT)
        pt0 = units(21, 2).rearrange("p (t h n) -> p t h n", t=T, h=H0)
        p0_place = sb("p0_place", [P, (T * H0 + 2) * N])
        p0 = p0_place[:, N:N + C].rearrange("p (h n) -> p h n", h=T * H0)
        p1_place = sb("p1_place", [P, (T * (H1 + 1) + 1) * N])
        p1 = p1_place[:, N:].rearrange("p (t a n) -> p t a n", t=T, a=H1 + 1)[:, :, 0:H1, :]
        vals = p1_place[:, 0:T * C].rearrange("p (t c) -> p t c", t=T)
        late_hi, late_lo = [w[:, WL:WG + 1].rearrange("p m k n -> p (m k n)").bitcast(F32) for w in (w_hi, w_lo)]

        def is_last_tile(t, g):
            return isinstance(g, int) and g == GROUPS - 1 and t == T - 1

        def scratch(t, g):
            return (units(13, 1), units(14, 1), units(15, 1)) if is_last_tile(t, g) else (s1, s2, s3)

        logit_rhs = [s.bitcast(BF16)[0:3 * PARTS1, 0:C] for s in (s2, s3)]
        staging = [s.rearrange("p (k n) -> p k n", k=KT)
                   for s in (units(0, 6), units(6, 6), late_hi, late_lo, units(0, 6), units(6, 6))]

        const_loaded = sem("const_loaded")
        columns_loaded = sem("columns_loaded")
        weight_loaded = [[sem(f"weight_loaded{m}_{half}") for half in range(2)] for m in range(6)]
        const_made = sem("const_made")
        eye_cleared = sem("eye_cleared")
        eye_made = sem("eye_made")
        rows_marked = sem("rows_marked")
        weight_top = [sem(f"weight_top{m}") for m in range(6)]
        weight_all = sem("weight_all")
        scale_step = sem("scale_step")
        weight_scaled = sem("weight_scaled")
        weight_hi = sem("weight_hi")
        weight_ready = sem("weight_ready")
        rows_loaded = sem("rows_loaded")
        x1_loaded = sem("x1_loaded")
        adj_loaded = sem("adj_loaded")
        out_stored = sem("out_stored")
        bias0_made = sem("bias0_made")
        not_adj_made = sem("not_adj_made")
        bn_done = [sem(f"bn_done{n}") for n in range(2)]
        mean_done = [sem(f"mean_done{n}") for n in range(2)]
        var_ready = [sem(f"var_ready{n}") for n in range(2)]
        rstd_ready = [sem(f"rstd_ready{n}") for n in range(2)]
        shift_ready = [sem(f"shift_ready{n}") for n in range(2)]
        rows0_ready = sem("rows0_ready")
        rows1_ready = sem("rows1_ready")
        t0_psum = sem("t0_psum")
        ht0_hi_ready = sem("ht0_hi_ready")
        ht0_ready = sem("ht0_ready")
        t1_psum = sem("t1_psum")
        ht1_hi_ready = sem("ht1_hi_ready")
        ht1_ready = sem("ht1_ready")
        q_psum = sem("q_psum")
        q_ready = sem("q_ready")
        k_psum = sem("k_psum")
        k_ready = sem("k_ready")
        v_psum = sem("v_psum")
        v_ready = sem("v_ready")
        s_psum = sem("s_psum")
        s_ready = sem("s_ready")
        max0_ready = sem("max0_ready")
        shifted0 = sem("shifted0")
        exp0_ready = sem("exp0_ready")
        sum0_ready = sem("sum0_ready")
        rinv0_ready = sem("rinv0_ready")
        p0_ready = sem("p0_ready")
        pt0_cleared = sem("pt0_cleared")
        pt0_psum = sem("pt0_psum")
        pt0_ready = sem("pt0_ready")
        ct_psum = sem("ct_psum")
        ct_hi_ready = sem("ct_hi_ready")
        ct_ready = sem("ct_ready")
        f_psum = sem("f_psum")
        bf_added = sem("bf_added")
        x1_ready = sem("x1_ready")
        kept = sem("kept")
        h_psum = sem("h_psum")
        h_hi_ready = sem("h_hi_ready")
        th_ready = sem("th_ready")
        h_ready = sem("h_ready")
        src_prod = sem("src_prod")
        dst_prod = sem("dst_prod")
        src_ready = sem("src_ready")
        dst_ready = sem("dst_ready")
        part1_ready = sem("part1_ready")
        rest_ready = sem("rest_ready")
        part2_ready = sem("part2_ready")
        parts_ready = sem("parts_ready")
        dst_terms_ready = sem("dst_terms_ready")
        lhs_psum = sem("lhs_psum")
        rhs_psum = sem("rhs_psum")
        logit_lhs_ready = sem("logit_lhs_ready")
        logit_rhs_ready = sem("logit_rhs_ready")
        g_psum = sem("g_psum")
        g_ready = sem("g_ready")
        gate_ready = sem("gate_ready")
        z_psum = sem("z_psum")
        z_ready = sem("z_ready")
        leaky_ready = sem("leaky_ready")
        masked1 = sem("masked1")
        max1_ready = sem("max1_ready")
        shifted1 = sem("shifted1")
        exp1_ready = sem("exp1_ready")
        sum1_ready = sem("sum1_ready")
        rinv1_ready = sem("rinv1_ready")
        rinv1_scaled = sem("rinv1_scaled")
        pt1_cleared = sem("pt1_cleared")
        pt1_psum = sem("pt1_psum")
        pt1_hi_ready = sem("pt1_hi_ready")
        pt1_ready = sem("pt1_ready")
        o_psum = sem("o_psum")
        o_norm = sem("o_norm")
        o_biased = sem("o_biased")
        o_min = sem("o_min")
        h_again = sem("h_again")
        o_exp = sem("o_exp")
        elu_ready = sem("elu_ready")
        diff_ready = sem("diff_ready")
        gated = sem("gated")
        summed = sem("summed")
        y_ready = sem("y_ready")

        block = ctx.enter_context(nc.Block())

        def columns(half):
            return slice(half * (C // 2), (half + 1) * (C // 2))

        def diagonal(pair, g):
            v = pair.rearrange("p (w n) -> p w n", n=P)
            return v[N * g:N * g + N, 1 - g:7 - g, N * g:N * g + N]

        def steps(eng, one):
            def flags(i):
                return [0 <= g < GROUPS for g in (i, i - 1, i - 2, i + 1)]
            for i in (0, 1):
                one(i, *flags(i))
            with eng.Fori(2, GROUPS - 1) as i:
                one(i, True, True, True, True)
            for i in range(GROUPS - 1, GROUPS + 2):
                one(i, *flags(i))

        @block.sync
        def _(sp):
            weights = [wq, wk, wv, wf, wl, wg]

            def load_weight(m):
                w = weights[m].rearrange("(k p) n -> p k n", p=P)
                for half in range(2):
                    sp.dma_start(staging[m][:, :, columns(half)], w[:, :, columns(half)])\
                        .then_inc(weight_loaded[m][half], DMA)

            sp.dma_start(rows, x_g[0]).then_inc(rows_loaded, DMA)
            load_weight(WQ)
            for dst, src in ((bq_col, bq), (bk_col, bk)):
                sp.dma_start(dst[:], src).then_inc(columns_loaded, DMA)
            load_weight(WK)
            load_weight(WV)
            sp.dma_start(x1, x_g[0]).then_inc(x1_loaded, DMA)
            for dst, src in ((bf_row, bf), (bv_row, bv), (bg_row, bg), (b1_row, b1)):
                sp.dma_start(dst[:], src.partition_broadcast(P)).then_inc(const_loaded, DMA)
            for dst, src in ((src_row, w_src), (dst_row, w_dst)):
                sp.dma_start(dst[:], src.rearrange("a e o -> (a e o)").partition_broadcast(P)).then_inc(const_loaded, DMA)
            load_weight(WF)
            sp.wait_ge(weight_ready, 2 * (WQ + 1))
            load_weight(WL)
            sp.wait_ge(weight_ready, 2 * (WK + 1))
            load_weight(WG)

            def one(i, now, mid, last, nxt):
                j, p = i - 1, i - 2
                if now:
                    after_alone(sp, eye_made, not_adj_made, i)
                    sp.dma_start(adj_u8[:], adj_g[i]).then_inc(adj_loaded, DMA)
                if last:
                    after_alone(sp, eye_made, y_ready, 2 * p + 1)
                    sp.dma_start(out_g[p, :, 0, :], keep[:, 0, :]).then_inc(out_stored, DMA)
                if nxt:
                    after_alone(sp, eye_made, t0_psum, 2 * i + 2)
                    if mid:
                        after_alone(sp, eye_made, t1_psum, 2 * j + 2)
                    sp.dma_start(rows, x_g[i + 1]).then_inc(rows_loaded, DMA)
                if last:
                    after_alone(sp, eye_made, y_ready, 2 * p + 2)
                    sp.dma_start(out_g[p, :, 1, :], keep[:, 1, :]).then_inc(out_stored, DMA)
                if now and mid:
                    after_alone(sp, eye_made, rows1_ready, 2 * j + 2)
                    after_alone(sp, eye_made, kept, j + 1)
                    sp.dma_start(x1, x_g[i]).then_inc(x1_loaded, DMA)

            steps(sp, one)
            sp.wait_ge(out_stored, 2 * DMA * GROUPS)

        @block.tensor
        def _(pe):
            def weight(m, k, part):
                return (w_hi, w_lo)[part][:, m, k, :]

            def project_rows(m, lhs, t, pair, done):
                for lo, hi in ((0, 512), (512, C)):
                    for k in range(KT):
                        for n, (a, b) in enumerate(((0, 0), (0, 1), (1, 0))):
                            mm = nc.tensor.matmul(pair[:, lo:hi], lhs(a, k), weight(m, k, b)[:, lo:hi],
                                                  start=(k == 0 and n == 0), stop=(k == KT - 1 and n == 2))
                mm.then_inc(done, 1)

            def project_columns(m, half, pair, done):
                for c in range(3):
                    o = (3 * half + c) * P
                    for k in range(KT):
                        for n, (a, b) in enumerate(((0, 0), (0, 1), (1, 0))):
                            mm = nc.tensor.matmul(pair[:, c * 256:(c + 1) * 256], weight(m, k, a)[:, o:o + P],
                                                  (ht0_hi, ht0_lo)[b][:, k, :],
                                                  start=(k == 0 and n == 0), stop=(k == KT - 1 and n == 2))
                mm.then_inc(done, 1)

            def transpose_rows(t, done):
                for k in range(KT):
                    mm = nc.tensor.transpose(pair_prj[t][:, k * P:(k + 1) * P], rows[:, t, k * P:(k + 1) * P], ident[:])
                mm.then_inc(done, 1)

            def transpose_windows(pair, place, block, done):
                for w in range(7):
                    c = (block + w) * N
                    mm = nc.tensor.transpose(pair_att[pair][:, w * P:(w + 1) * P], place[:, c:c + 2 * N], ident[:])
                mm.then_inc(done, 1)

            def transpose_p1(t, half):
                transpose_windows(half, p1_place, t * (H1 + 1) + 6 * half, pt1_psum)

            def attend1(t):
                for a in range(H1):
                    c = slice(a * E1, (a + 1) * E1)
                    parts = ((pt1_hi, h1v_hi), (pt1_hi, h1v_lo), (pt1_lo, h1v_hi))
                    for n, (pt, hv) in enumerate(parts):
                        mm = nc.tensor.matmul(pair_att[t][:, c], pt[:, a, :], hv[:, t, c], start=(n == 0), stop=(n == 2))
                mm.then_inc(o_psum, 1)

            pe.wait_ge(eye_made, 2)
            for t in range(T):
                pe.wait_ge(rows0_ready, t + 1)
                transpose_rows(t, t0_psum)

            def one(i, now, mid, last, nxt):
                j, p = i - 1, i - 2
                first = isinstance(i, int) and i == 0
                first_mid = isinstance(i, int) and i == 1
                tail = mid and not now

                def project_h(t):
                    pe.wait_ge(ht1_ready, 2 * j + t + 1)
                    if now:
                        pe.wait_ge(v_ready, 2 * i + t + 1)
                    project_rows(WL, lambda a, k: (ht1_hi, ht1_lo)[a][:, k, t * P:(t + 1) * P], t,
                                 pair_prj[t], h_psum)

                if now:
                    if first:
                        pe.wait_ge(weight_ready, 2 * WQ + 1)
                    pe.wait_ge(ht0_ready, 2 * i + 2)
                    after(pe, x1_ready, 2 * i - 1)
                    project_columns(WQ, 0, pair_prj[0], q_psum)
                if last:
                    pe.wait_ge(exp1_ready, 2 * p + 1)
                    transpose_p1(0, 0)
                    pe.wait_ge(z_ready, 2 * p + 2)
                    transpose_p1(0, 1)
                if now:
                    if first:
                        pe.wait_ge(weight_ready, 2 * WQ + 2)
                    after(pe, x1_ready, 2 * i)
                    project_columns(WQ, 1, pair_prj[1], q_psum)
                if tail:
                    for t in range(T):
                        pe.wait_ge(rows1_ready, 2 * j + t + 1)
                        transpose_rows(t, t1_psum)
                if last:
                    pe.wait_ge(h_ready, 2 * p + 2)
                    pe.wait_ge(pt1_ready, 4 * p + 2)
                    attend1(0)
                if now:
                    if first:
                        pe.wait_ge(weight_ready, 2 * WK + 1)
                    pe.wait_ge(q_ready, 2 * i + 1)
                    project_columns(WK, 0, pair_prj[0], k_psum)
                if last:
                    pe.wait_ge(exp1_ready, 2 * p + 2)
                    pe.wait_ge(o_norm, 2 * p + 1)
                    transpose_p1(1, 0)
                    transpose_p1(1, 1)
                if now:
                    if first:
                        pe.wait_ge(weight_ready, 2 * WK + 2)
                    pe.wait_ge(q_ready, 2 * i + 2)
                    project_columns(WK, 1, pair_prj[1], k_psum)
                if tail:
                    project_h(0)
                if last:
                    pe.wait_ge(pt1_ready, 4 * p + 4)
                    attend1(1)

                if mid and not tail:
                    for t in range(T):
                        pe.wait_ge(rows1_ready, 2 * j + t + 1)
                        if now:
                            pe.wait_ge(k_ready, 2 * i + t + 1)
                        transpose_rows(t, t1_psum)

                if now:
                    pe.wait_ge(k_ready, 2 * i + 2)
                    for t in range(T):
                        if last and t == 0:
                            pe.wait_ge(pt1_ready, 4 * p + 3)
                        elif last:
                            pe.wait_ge(o_norm, 2 * p + 2)
                        else:
                            after(pe, ct_ready, 2 * i - 1 + t)
                        for h in range(H0):
                            mm = nc.tensor.matmul(pair_att[t][:, h * P:(h + 1) * P], qt[:, h, t * P:(t + 1) * P],
                                                  kt[:, h, t * P:(t + 1) * P], start=True, stop=True)
                        mm.then_inc(s_psum, 1)

                    if first:
                        pe.wait_ge(weight_ready, 2 * WV + 2)
                    for t in range(T):
                        if mid:
                            pe.wait_ge(ht1_ready, 2 * j + t + 1)
                        else:
                            pe.wait_ge(k_ready, 2 * i + t + 1)
                        project_rows(WV, lambda a, k: (ht0_hi, ht0_lo)[a][:, k, t * P:(t + 1) * P], t,
                                     pair_prj[t], v_psum)

                if mid:
                    if first_mid:
                        pe.wait_ge(weight_ready, 2 * WL + 2)
                    if not tail:
                        project_h(0)
                    project_h(1)

                if now:
                    pe.wait_ge(p0_ready, i + 1)
                    for t in range(T):
                        transpose_windows(t, p0_place, t * H0, pt0_psum)

                for t in range(T):
                    if nxt:
                        pe.wait_ge(rows0_ready, 2 * i + t + 3)
                        if mid:
                            pe.wait_ge(h_ready, 2 * j + t + 1)
                        else:
                            pe.wait_ge(v_ready, 2 * i + t + 1)
                        transpose_rows(t, t0_psum)
                    if now:
                        pe.wait_ge(v_ready, 2 * i + t + 1)
                        pe.wait_ge(pt0_ready, 2 * i + t + 1)
                        for h in range(H0):
                            mm = nc.tensor.matmul(pair_att[t][:, h * P:(h + 1) * P], vals[:, t, h * P:(h + 1) * P],
                                                  pt0[:, t, h, :], start=True, stop=True)
                        mm.then_inc(ct_psum, 1)

                def logit_operands():
                    pe.wait_ge(dst_terms_ready, j + 1)
                    for t in range(T):
                        if now:
                            pe.wait_ge(ct_ready, 2 * i + t + 1)
                        elif last and t == 0:
                            pe.wait_ge(pt1_ready, 4 * p + 3)
                        elif last:
                            pe.wait_ge(o_norm, 2 * p + 2)
                        nc.tensor.matmul(pair_att[t][0:PARTS1, 0:P], parts[:, t, 0, :], ident_bf[:],
                                         start=True, stop=True).then_inc(lhs_psum, 1)
                        nc.tensor.matmul(pair_att[t][0:3 * PARTS1, 512:512 + N], dst_terms[:, t, :], node_eye[:],
                                         start=True, stop=True).then_inc(rhs_psum, 1)

                if mid:
                    if first_mid:
                        pe.wait_ge(weight_ready, 2 * WG + 2)
                        pe.wait_ge(rows_marked, 4 + T)
                    for t in range(T):
                        if nxt:
                            pe.wait_ge(ht0_ready, 2 * i + t + 3)
                        else:
                            pe.wait_ge(h_ready, 2 * j + t + 1)
                        project_rows(WG, lambda a, k: (ht1_hi, ht1_lo)[a][:, k, t * P:(t + 1) * P], t,
                                     pair_prj[t], g_psum)
                        if t == (1 if tail else 0):
                            logit_operands()

                    for t in range(T):
                        pe.wait_ge(logit_lhs_ready, 2 * j + t + 1)
                        pe.wait_ge(logit_rhs_ready, 2 * j + t + 1)
                        for lo, hi in ((0, 512), (512, C)):
                            mm = nc.tensor.matmul(pair_att[t][:, lo:hi], logit_lhs[0:3 * PARTS1, t, :],
                                                  logit_rhs[t][:, lo:hi], start=True, stop=True)
                        mm.then_inc(z_psum, 1)

                if now:
                    if first:
                        pe.wait_ge(weight_ready, 2 * WF + 2)
                    for t in range(T):
                        pe.wait_ge(ct_ready, 2 * i + t + 1)
                        if mid:
                            pe.wait_ge(g_ready, 2 * j + t + 1)
                        else:
                            pe.wait_ge(ht0_ready, 2 * i + t + 3)
                        project_rows(WF, lambda a, k: (ct_hi, ct_lo)[a][:, t, k, :], t, pair_prj[t], f_psum)

            steps(pe, one)

        @block.vector
        def _(dve):
            made = [0]

            def scale(ins):
                made[0] += 1
                ins.then_inc(scale_step, 1)
                dve.wait_ge(scale_step, made[0])

            def col(tensor, n):
                return tensor[:, n:n + 1]

            def power_of_two(dst, src):
                scale(nc.vector.tensor_scalar(dst.bitcast(U32), src.bitcast(U32), EXPONENT, None, ALU.bitwise_and))
                scale(nc.vector.tensor_scalar(dst, dst, TINY, None, ALU.max))

            def largest(m, half):
                dve.wait_ge(weight_loaded[m][half], DMA)
                nc.vector.tensor_reduce(w_top[:, m, half:half + 1], staging[m][:, :, columns(half)], AX_XY, ALU.max,
                                        apply_absolute_value=True).then_inc(weight_top[m], 1)

            def scale_weight(m):
                dve.wait_ge(weight_all, m + 1)
                scale(nc.vector.tensor_tensor(col(w_pow, m), w_all[:, m, 0:1], w_all[:, m, 1:2],
                                              ALU.max if m in BY_LARGEST else ALU.add))
                power_of_two(col(w_pow, m), col(w_pow, m))
                scale(nc.vector.reciprocal(col(w_rec, m), col(w_pow, m)))
                nc.vector.tensor_scalar(col(w_scale, m), col(w_rec, m), W_TOP, None, ALU.mult).then_inc(weight_scaled, 1)
                undo = 1.0 / W_TOP if m == WF else 1.0 / (W_TOP * HN)
                scale(nc.vector.tensor_scalar(col(w_undo, m), col(w_pow, m), undo, None, ALU.mult))
                if m == WV:
                    dve.wait_ge(const_loaded, 6 * DMA)
                    scale(nc.vector.tensor_reduce(col(w_pow, 6), bv_row[:], AX_X, ALU.max, apply_absolute_value=True))
                    power_of_two(col(w_pow, 6), col(w_pow, 6))
                    scale(nc.vector.tensor_scalar(col(v_bound, 0), col(w_pow, 6), 2.0, None, ALU.mult))
                    scale(nc.vector.scalar_tensor_tensor(col(v_bound, 0), col(w_pow, WV), 2048.0, col(v_bound, 0),
                                                         ALU.mult, ALU.add))
                    power_of_two(col(v_bound, 1), col(v_bound, 0))
                    scale(nc.vector.reciprocal(col(v_bound, 2), col(v_bound, 1)))
                    scale(nc.vector.tensor_scalar(col(v_bound, 2), col(v_bound, 2), V_TOP, None, ALU.mult))
                    scale(nc.vector.tensor_scalar(bv_row[:], bv_row[:], col(v_bound, 2), None, ALU.mult))
                    scale(nc.vector.tensor_tensor(col(w_undo, WV), col(w_undo, WV), col(v_bound, 2), ALU.mult))
                if m == WF:
                    scale(nc.vector.tensor_scalar(col(v_bound, 3), col(v_bound, 1), 1.0 / V_TOP, None, ALU.mult))
                    scale(nc.vector.tensor_tensor(col(w_undo, WF), col(w_undo, WF), col(v_bound, 3), ALU.mult))
                if m == WL:
                    scale(nc.vector.tensor_scalar(col(w_undo, 7), col(w_undo, WL), 1.0 / HV, None, ALU.mult))

            def low_weight(m, half):
                dve.wait_ge(weight_hi, 2 * m + half + 1)
                nc.vector.scalar_tensor_tensor(w_lo[:, m, :, columns(half)], staging[m][:, :, columns(half)],
                                               col(w_scale, m), w_hi[:, m, :, columns(half)],
                                               ALU.mult, ALU.subtract).then_inc(weight_ready, 1)

            def statistics(n, src, g):
                for t in range(T):
                    for c in range(2):
                        bn = nc.vector.bn_stats(bn_out[n][:, t, c, :], src[:, t, c * (C // 2):(c + 1) * (C // 2)])
                bn.then_inc(bn_done[n], 1)
                after_alone(dve, eye_made, bn_done[n], g + 1)
                for t in range(T):
                    ag = nc.vector.bn_aggr(mean_var[n][:, t, :], bn_out[n][:, t].rearrange("p c s -> p (c s)"))
                ag.then_inc(mean_done[n], 1)
                dve.wait_ge(mean_done[n], g + 1)
                nc.vector.tensor_scalar(var_eps[n][:], mean_var[n][:, :, 1], EPS, 1.0 / (HN * HN), ALU.add, ALU.mult)\
                    .then_inc(var_ready[n], 1)
                dve.wait_ge(rstd_ready[n], g + 1)
                nc.vector.scalar_tensor_tensor(shift[n][:], mean_var[n][:, :, 0], -1.0, rstd[n][:],
                                               ALU.mult, ALU.mult).then_inc(shift_ready[n], 1)

            def low_part_transposed(t, g, hi_t, lo_t, hi_ready, ready):
                dve.wait_ge(hi_ready, 2 * g + t + 1)
                nc.vector.tensor_tensor(lo_t[:, :, t * P:(t + 1) * P],
                                        pair_prj[t][:, 0:C].rearrange("p (k n) -> p k n", k=KT),
                                        hi_t[:, :, t * P:(t + 1) * P], ALU.subtract).then_inc(ready, 1)

            def biased_columns(half, pair, dst, bias, m, ready):
                nc.vector.scalar_tensor_tensor(
                    dst[:, 3 * half:3 * half + 3, :], pair[:, 0:C].rearrange("p (c n) -> p c n", c=3), col(w_undo, m),
                    bias[:, 3 * half:3 * half + 3].unsqueeze(2).broadcast_to([P, 3, 2 * P]),
                    ALU.mult, ALU.add).then_inc(ready, 1)

            def pt1_low(t, half, p):
                dve.wait_ge(pt1_hi_ready, 4 * p + 2 * t + half + 1)
                heads = slice(6 * half, 6 * half + 6)
                for g in range(2):
                    r = slice(N * g, N * g + N)
                    lo = nc.vector.tensor_tensor(
                        pt1_lo[r, heads, r], diagonal(pair_att[half][:], g), pt1_hi[r, heads, r], ALU.subtract)
                lo.then_inc(pt1_ready, 1)

            def sum_and_invert(t, g):
                n = 2 * g + t + 1
                dve.wait_ge(exp1_ready, n)
                nc.vector.tensor_reduce(sum1[:, t, :], p1[:, t], AX_X, ALU.add).then_inc(sum1_ready, 1)
                dve.wait_ge(sum1_ready, n)
                nc.vector.reciprocal(rinv1[:, t, :], sum1[:, t, :]).then_inc(rinv1_ready, 1)
                dve.wait_ge(rinv1_ready, n)
                nc.vector.tensor_scalar(rinv1[:, t, :], rinv1[:, t, :], col(w_undo, 7), None, ALU.mult)\
                    .then_inc(rinv1_scaled, 1)

            def heads1(ap):
                return ap.rearrange("p (a n) -> p a n", a=H1)

            def output_first(t, p):
                s1, s2, s3 = scratch(t, p)
                dve.wait_ge(rinv1_scaled, 2 * p + t + 1)
                dve.wait_ge(o_psum, 2 * p + t + 1)
                nc.vector.tensor_tensor(heads1(s1), heads1(pair_att[t][:, 0:C]),
                                        rinv1[:, t, :].unsqueeze(2).broadcast_to([P, H1, E1]), ALU.mult)\
                    .then_inc(o_norm, 1)

            def output_min(t, p):
                s1, s2, s3 = scratch(t, p)
                dve.wait_ge(o_biased, 2 * p + t + 1)
                nc.vector.tensor_scalar(s2, s1, 0.0, None, ALU.min).then_inc(o_min, 1)

            def output_last(t, p):
                s1, s2, s3 = scratch(t, p)
                n = 2 * p + t + 1
                dve.wait_ge(o_exp, n)
                nc.vector.scalar_tensor_tensor(s1, s2, -1.0, s1, ALU.add, ALU.max).then_inc(elu_ready, 1)
                dve.wait_ge(elu_ready, n)
                dve.wait_ge(h_again, n)
                nc.vector.tensor_tensor(s2, s1, s3, ALU.subtract).then_inc(diff_ready, 1)
                dve.wait_ge(diff_ready, n)
                dve.wait_ge(gate_ready, n)
                nc.vector.scalar_tensor_tensor(s2, gate[:, t, :], 1.0, s2, ALU.add, ALU.mult).then_inc(gated, 1)
                dve.wait_ge(gated, n)
                nc.vector.scalar_tensor_tensor(keep[:, t, :], s2, 0.5, keep[:, t, :], ALU.mult, ALU.add)\
                    .then_inc(summed, 1)

            dve.wait_ge(eye_made, 1)
            nc.vector.tensor_copy(ident_bf[:], ident[:]).then_inc(rows_marked, 1)
            nc.vector.tensor_reduce(of_head[:], ident[:, 0:3 * PARTS1].rearrange("p (q a) -> p a q", a=H1), AX_X,
                                    ALU.add).then_inc(rows_marked, 1)
            nc.vector.tensor_reduce(of_graph[:], ident[:, PARTS1:3 * PARTS1].rearrange("p (g q) -> p g q", g=2), AX_X,
                                    ALU.add).then_inc(rows_marked, 1)
            for t in range(T):
                nc.vector.tensor_scalar(dst_terms[:, t, :], ident[:, 0:3 * PARTS1], 0.0, 0.5, ALU.mult, ALU.add)\
                    .then_inc(rows_marked, 1)
            dve.wait_ge(rows_marked, 3 + T)
            nc.vector.tensor_copy(logit_lhs[:].rearrange("p t (g n) -> p t g n", g=2),
                                  of_graph[:].unsqueeze(1).unsqueeze(3).broadcast_to([P, T, 2, N]))\
                .then_inc(rows_marked, 1)
            dve.wait_ge(eye_cleared, 4)
            dve.wait_ge(rows_loaded, DMA)
            statistics(0, rows, 0)
            scale_weight(WQ)
            low_weight(WQ, 0)
            for t in range(T):
                low_part_transposed(t, 0, ht0_hi, ht0_lo, ht0_hi_ready, ht0_ready)
            low_weight(WQ, 1)
            largest(WV, 0)
            scale_weight(WK)
            largest(WV, 1)
            low_weight(WK, 0)
            dve.wait_ge(columns_loaded, 2 * DMA)

            def one(i, now, mid, last, nxt):
                j, p = i - 1, i - 2
                first = isinstance(i, int) and i == 0
                tail, final = mid and not now, last and not mid
                if mid:
                    dve.wait_ge(x1_ready, 2 * j + 2)
                    statistics(1, x1, j)
                if now:
                    dve.wait_ge(q_psum, 2 * i + 1)
                    biased_columns(0, pair_prj[0], qt, bq_col, WQ, q_ready)
                if isinstance(i, int) and i == 1:
                    for half in range(2):
                        low_weight(WG, half)
                if first:
                    low_weight(WK, 1)
                    scale_weight(WV)
                if last:
                    pt1_low(0, 0, p)
                    pt1_low(0, 1, p)
                if now:
                    dve.wait_ge(q_psum, 2 * i + 2)
                    biased_columns(1, pair_prj[1], qt, bq_col, WQ, q_ready)
                if first:
                    low_weight(WV, 0)
                if tail:
                    low_part_transposed(0, j, ht1_hi, ht1_lo, ht1_hi_ready, ht1_ready)
                    low_part_transposed(1, j, ht1_hi, ht1_lo, ht1_hi_ready, ht1_ready)
                if last:
                    output_first(0, p)
                    output_min(0, p)
                if final:
                    sum_and_invert(1, p)
                if now:
                    dve.wait_ge(k_psum, 2 * i + 1)
                    biased_columns(0, pair_prj[0], kt, bk_col, WK, k_ready)
                if first:
                    low_weight(WV, 1)
                    scale_weight(WF)
                if last:
                    if tail or final:
                        pt1_low(1, 0, p)
                        pt1_low(1, 1, p)
                        output_last(0, p)
                    else:
                        output_last(0, p)
                        pt1_low(1, 0, p)
                        pt1_low(1, 1, p)
                if now:
                    dve.wait_ge(k_psum, 2 * i + 2)
                    biased_columns(1, pair_prj[1], kt, bk_col, WK, k_ready)
                if last:
                    output_first(1, p)
                if mid and not tail:
                    low_part_transposed(0, j, ht1_hi, ht1_lo, ht1_hi_ready, ht1_ready)
                if last:
                    output_min(1, p)
                if mid and not tail:
                    low_part_transposed(1, j, ht1_hi, ht1_lo, ht1_hi_ready, ht1_ready)
                if last:
                    output_last(1, p)

                if now:
                    dve.wait_ge(adj_loaded, DMA * (i + 1))
                    nc.vector.tensor_scalar(bias0[:], adj_u8[:], -1.0, NEG_L0, ALU.add, ALU.mult).then_inc(bias0_made, 1)
                    dve.wait_ge(bias0_made, i + 1)
                    for t in range(T):
                        dve.wait_ge(s_psum, 2 * i + t + 1)
                        for g in range(2):
                            r = slice(N * g, N * g + N)
                            sc = nc.vector.scalar_tensor_tensor(
                                p0[r, t * H0:(t + 1) * H0, :],
                                pair_att[t][r, 0:C].rearrange("p (h n) -> p h n", h=H0)[:, :, r], INV_SQRT_D,
                                bias0[r, t, :].unsqueeze(1).broadcast_to([N, H0, N]), ALU.mult, ALU.add)
                        sc.then_inc(s_ready, 1)
                    wide = [P, T * H0, N]
                    dve.wait_ge(s_ready, 2 * i + 2)
                    nc.vector.tensor_reduce(max0[:], p0, AX_X, ALU.max).then_inc(max0_ready, 1)
                    dve.wait_ge(max0_ready, i + 1)
                    nc.vector.tensor_tensor(p0, p0, max0[:].unsqueeze(2).broadcast_to(wide), ALU.subtract)\
                        .then_inc(shifted0, 1)

                    if first:
                        low_weight(WF, 0)
                    dve.wait_ge(v_psum, 2 * i + 1)
                    nc.vector.scalar_tensor_tensor(vals[:, 0, :], pair_prj[0][:, 0:C], col(w_undo, WV), bv_row[:],
                                                   ALU.mult, ALU.add).then_inc(v_ready, 1)
                    dve.wait_ge(exp0_ready, i + 1)
                    nc.vector.tensor_reduce(sum0[:], p0, AX_X, ALU.add).then_inc(sum0_ready, 1)
                    dve.wait_ge(sum0_ready, i + 1)
                    nc.vector.reciprocal(rinv0[:], sum0[:]).then_inc(rinv0_ready, 1)
                    dve.wait_ge(rinv0_ready, i + 1)
                    nc.vector.tensor_tensor(p0, p0, rinv0[:].unsqueeze(2).broadcast_to(wide), ALU.mult)\
                        .then_inc(p0_ready, 1)
                    if first:
                        low_weight(WF, 1)
                        dve.wait_ge(rows_loaded, DMA * (i + 2))
                        statistics(0, rows, i + 1)
                    dve.wait_ge(v_psum, 2 * i + 2)
                    nc.vector.scalar_tensor_tensor(vals[:, 1, :], pair_prj[1][:, 0:C], col(w_undo, WV), bv_row[:],
                                                   ALU.mult, ALU.add).then_inc(v_ready, 1)
                if nxt and not first:
                    dve.wait_ge(rows_loaded, DMA * (i + 2))
                    statistics(0, rows, i + 1)

                def h_low(t):
                    dve.wait_ge(th_ready, 2 * j + t + 1)
                    nc.vector.scalar_tensor_tensor(h1v_lo[:, t, :], pair_prj[t][:, 0:C], HV, h1v_hi[:, t, :],
                                                   ALU.mult, ALU.subtract).then_inc(h_ready, 1)

                def source_and_target(t):
                    dve.wait_ge(src_prod, 2 * j + t + 1)
                    nc.vector.tensor_reduce(src_dst[:, t, 0, :], heads1(s2), AX_X, ALU.add).then_inc(src_ready, 1)
                    dve.wait_ge(dst_prod, 2 * j + t + 1)
                    nc.vector.tensor_reduce(src_dst[:, t, 1, :], heads1(s3), AX_X, ALU.add).then_inc(dst_ready, 1)

                if mid:
                    h_low(0)
                    source_and_target(0)
                    h_low(1)
                if nxt:
                    for t in range(T):
                        low_part_transposed(t, i + 1, ht0_hi, ht0_lo, ht0_hi_ready, ht0_ready)
                if now:
                    for t in range(T):
                        dve.wait_ge(ct_hi_ready, 2 * i + t + 1)
                        nc.vector.tensor_tensor(ct_lo[:, t].rearrange("p k n -> p (k n)"), pair_att[t][:, 0:C],
                                                ct_hi[:, t].rearrange("p k n -> p (k n)"), ALU.subtract)\
                            .then_inc(ct_ready, 1)
                if first:
                    largest(WL, 0)
                    largest(WL, 1)

                def keep_x1(t):
                    dve.wait_ge(bf_added, 2 * i + t + 1)
                    dve.wait_ge(f_psum, 2 * i + t + 1)
                    nc.vector.scalar_tensor_tensor(x1[:, t, :], pair_prj[t][:, 0:C], col(w_undo, WF), x1[:, t, :],
                                                   ALU.mult, ALU.add).then_inc(x1_ready, 1)

                def split_source_and_target():
                    whole = src_dst[:].rearrange("p t s a -> p (t s) a")
                    left = rest[:].rearrange("p t s a -> p (t s) a")
                    part = parts[:].rearrange("p t s (k a) -> p (t s) k a", k=3)
                    dve.wait_ge(src_ready, 2 * j + 2)
                    dve.wait_ge(dst_ready, 2 * j + 2)
                    nc.vector.tensor_copy(part[:, :, 0, :], whole).then_inc(part1_ready, 1)
                    dve.wait_ge(part1_ready, j + 1)
                    nc.vector.tensor_tensor(left, whole, part[:, :, 0, :], ALU.subtract).then_inc(rest_ready, 1)
                    dve.wait_ge(rest_ready, j + 1)
                    nc.vector.tensor_copy(part[:, :, 1, :], left).then_inc(part2_ready, 1)
                    dve.wait_ge(part2_ready, j + 1)
                    nc.vector.tensor_tensor(part[:, :, 2, :], left, part[:, :, 1, :], ALU.subtract)\
                        .then_inc(parts_ready, 1)

                def spread_over_heads(t):
                    dve.wait_ge(rhs_psum, 2 * j + t + 1)
                    rows_of = slice(0, 3 * PARTS1)
                    nc.vector.tensor_tensor(
                        logit_rhs[t].rearrange("p (a n) -> p a n", a=H1),
                        pair_att[t][rows_of, 512:512 + N].unsqueeze(1).broadcast_to([3 * PARTS1, H1, N]),
                        of_head[rows_of, :].unsqueeze(2).broadcast_to([3 * PARTS1, H1, N]), ALU.mult)\
                        .then_inc(logit_rhs_ready, 1)

                def mask_and_shift(t):
                    n = 2 * j + t + 1
                    dve.wait_ge(z_ready, n)
                    nc.vector.scalar_tensor_tensor(p1[:, t], p1[:, t], ALPHA, p1[:, t], ALU.mult, ALU.max)\
                        .then_inc(leaky_ready, 1)
                    after_alone(dve, eye_made, leaky_ready, n)
                    nc.vector.copy_predicated(p1[:, t], not_adj[:, t, :].unsqueeze(1).broadcast_to([P, H1, N]),
                                              neg_l1[:].unsqueeze(2).broadcast_to([P, H1, N])).then_inc(masked1, 1)
                    dve.wait_ge(masked1, n)
                    nc.vector.tensor_reduce(max1[:, t, :], p1[:, t], AX_X, ALU.max).then_inc(max1_ready, 1)
                    dve.wait_ge(max1_ready, n)
                    nc.vector.tensor_tensor(p1[:, t], p1[:, t], max1[:, t, :].unsqueeze(2).broadcast_to([P, H1, N]),
                                            ALU.subtract).then_inc(shifted1, 1)

                if mid:
                    source_and_target(1)
                    split_source_and_target()
                    for t in range(T):
                        dve.wait_ge(g_psum, 2 * j + t + 1)
                        nc.vector.scalar_tensor_tensor(gate[:, t, :], pair_prj[t][:, 0:C], col(w_undo, WG), bg_row[:],
                                                       ALU.mult, ALU.add).then_inc(g_ready, 1)
                        if t == (1 if tail else 0):
                            spread_over_heads(0)
                            spread_over_heads(1)
                    after_alone(dve, eye_made, not_adj_made, j + 1)
                    mask_and_shift(0)
                if now:
                    keep_x1(0)
                if first:
                    scale_weight(WL)
                if mid:
                    mask_and_shift(1)
                    sum_and_invert(0, j)
                if now:
                    keep_x1(1)
                if mid and not tail:
                    sum_and_invert(1, j)
                if now:
                    after(dve, masked1, 2 * j + 2)
                    nc.vector.tensor_scalar(not_adj[:], adj_u8[:], -1.0, 1.0, ALU.mult, ALU.add)\
                        .then_inc(not_adj_made, 1)
                if first:
                    scale_weight(WG)
                    for half in range(2):
                        low_weight(WL, half)

            steps(dve, one)

        @block.scalar
        def _(act):
            def magnitudes(m, half):
                act.wait_ge(weight_loaded[m][half], DMA)
                nc.scalar.activation(w_hi[:, m, :, columns(half)], staging[m][:, :, columns(half)], ACT.Abs,
                                     accum_out=w_top[:, m, half:half + 1]).then_inc(weight_top[m], 1)

            def high_weight(m, half):
                act.wait_ge(weight_scaled, m + 1)
                nc.scalar.activation(w_hi[:, m, :, columns(half)], staging[m][:, :, columns(half)], ACT.Copy,
                                     scale=w_scale[:, m:m + 1]).then_inc(weight_hi, 1)

            def normalise(n, src, ready):
                for t in range(T):
                    nc.scalar.activation(rows[:, t, :], src[:, t, :], ACT.Relu, bias=shift[n][:, t:t + 1],
                                         scale=rstd[n][:, t:t + 1]).then_inc(ready, 1)

            def high_part_transposed(t, g, psum, hi_t, hi_ready):
                act.wait_ge(psum, 2 * g + t + 1)
                nc.scalar.activation(hi_t[:, :, t * P:(t + 1) * P],
                                     pair_prj[t][:, 0:C].rearrange("p (k n) -> p k n", k=KT), ACT.Copy)\
                    .then_inc(hi_ready, 1)

            def pt1_high(t, half, p):
                act.wait_ge(pt1_psum, 4 * p + 2 * t + half + 1)
                for g in range(2):
                    r = slice(N * g, N * g + N)
                    hi = nc.scalar.activation(
                        pt1_hi[r, 6 * half:6 * half + 6, r], diagonal(pair_att[half][:], g), ACT.Copy)
                hi.then_inc(pt1_hi_ready, 1)

            def exponentials1(t, g):
                act.wait_ge(shifted1, 2 * g + t + 1)
                nc.scalar.activation(p1[:, t], p1[:, t], ACT.Exp).then_inc(exp1_ready, 1)

            def output_parts(t, p):
                s1, s2, s3 = scratch(t, p)
                if not is_last_tile(t, p):
                    after(act, y_ready, 2 * p + t)
                act.wait_ge(kept, p + 1)
                nc.scalar.activation(s3, keep[:, t, :], ACT.Relu, bias=keep_shift[:, t:t + 1],
                                     scale=keep_rstd[:, t:t + 1]).then_inc(h_again, 1)
                act.wait_ge(o_min, 2 * p + t + 1)
                nc.scalar.activation(s2, s2, ACT.Exp).then_inc(o_exp, 1)

            act.wait_ge(const_made, 6)
            magnitudes(WQ, 0)
            act.wait_ge(shift_ready[0], 1)
            normalise(0, rows, rows0_ready)
            magnitudes(WQ, 1)
            high_weight(WQ, 0)
            for t in range(T):
                high_part_transposed(t, 0, t0_psum, ht0_hi, ht0_hi_ready)
            high_weight(WQ, 1)
            for half in range(2):
                magnitudes(WK, half)
            for m in (WK, WV):
                for half in range(2):
                    high_weight(m, half)
            for half in range(2):
                magnitudes(WF, half)
            for half in range(2):
                high_weight(WF, half)

            def one(i, now, mid, last, nxt):
                j, p = i - 1, i - 2
                first = isinstance(i, int) and i == 0
                tail, final = mid and not now, last and not mid
                if isinstance(i, int) and i == 2:
                    act.wait_ge(pt1_cleared, 1)
                if tail:
                    pt1_high(0, 0, p)
                    pt1_high(0, 1, p)
                if mid:
                    act.wait_ge(shift_ready[1], j + 1)
                    act.wait_ge(t0_psum, 2 * i + 2 if now else 2 * GROUPS)
                    normalise(1, x1, rows1_ready)
                if last and not tail:
                    pt1_high(0, 0, p)
                    pt1_high(0, 1, p)
                    if final:
                        exponentials1(1, p)
                    output_parts(0, p)
                    pt1_high(1, 0, p)
                    pt1_high(1, 1, p)
                if mid:
                    if isinstance(i, int) and i == 1:
                        act.wait_ge(weight_ready, 12)
                    for t in range(T):
                        high_part_transposed(t, j, t1_psum, ht1_hi, ht1_hi_ready)
                if tail:
                    output_parts(0, p)
                    pt1_high(1, 0, p)
                    pt1_high(1, 1, p)
                if last:
                    output_parts(1, p)
                if now:
                    act.wait_ge(shifted0, i + 1)
                    nc.scalar.activation(p0, p0, ACT.Exp).then_inc(exp0_ready, 1)
                if now:
                    act.wait_ge(s_psum, 2 * i + 2)
                    nc.scalar.activation(units(21, 2), zero[:].broadcast_to([P, 2 * C]), ACT.Copy)\
                        .then_inc(pt0_cleared, 1)
                if nxt:
                    act.wait_ge(shift_ready[0], i + 2)
                    normalise(0, rows, rows0_ready)

                def h_high(t):
                    act.wait_ge(h_psum, 2 * j + t + 1)
                    nc.scalar.activation(h1v_hi[:, t, :], pair_prj[t][:, 0:C], ACT.Copy, scale=HV)\
                        .then_inc(h_hi_ready, 1)

                def h_tanh(t):
                    if t == 0:
                        after(act, diff_ready, 2 * p + 2)
                    else:
                        act.wait_ge(dst_prod, 2 * j + 1)
                    nc.scalar.activation(s1, pair_prj[t][:, 0:C], ACT.Tanh, scale=w_undo[:, WL:WL + 1])\
                        .then_inc(th_ready, 1)

                def probabilities_transposed(t):
                    act.wait_ge(pt0_psum, 2 * i + t + 1)
                    for g in range(2):
                        r = slice(N * g, N * g + N)
                        pt = nc.scalar.activation(pt0[r, t, :, r], diagonal(pair_att[t][:], g), ACT.Copy)
                    pt.then_inc(pt0_ready, 1)

                if mid:
                    h_high(0)
                    h_tanh(0)
                    h_high(1)
                if now:
                    act.wait_ge(pt0_cleared, i + 1)
                    probabilities_transposed(0)
                if mid:
                    h_tanh(1)
                if now:
                    probabilities_transposed(1)
                if nxt:
                    for t in range(T):
                        high_part_transposed(t, i + 1, t0_psum, ht0_hi, ht0_hi_ready)
                if now:
                    for t in range(T):
                        act.wait_ge(ct_psum, 2 * i + t + 1)
                        nc.scalar.activation(ct_hi[:, t].rearrange("p k n -> p (k n)"), pair_att[t][:, 0:C], ACT.Copy)\
                            .then_inc(ct_hi_ready, 1)
                if first:
                    act.wait_ge(weight_ready, 2 * (WV + 1))
                    for half in range(2):
                        magnitudes(WG, half)
                def gates():
                    for t in range(T):
                        act.wait_ge(g_ready, 2 * j + t + 1)
                        nc.scalar.activation(gate[:, t, :], gate[:, t, :], ACT.Tanh, scale=0.5).then_inc(gate_ready, 1)

                if mid:
                    if tail:
                        gates()
                    for t in range(T):
                        act.wait_ge(lhs_psum, 2 * j + t + 1)
                        nc.scalar.activation(logit_lhs[0:PARTS1, t, :], pair_att[t][0:PARTS1, 0:P], ACT.Copy)\
                            .then_inc(logit_lhs_ready, 1)
                    for t in range(T):
                        act.wait_ge(z_psum, 2 * j + t + 1)
                        nc.scalar.activation(p1[:, t], pair_att[t][:, 0:C].rearrange("p (a n) -> p a n", a=H1), ACT.Copy)\
                            .then_inc(z_ready, 1)
                    if not tail:
                        gates()
                    exponentials1(0, j)
                    if not tail:
                        exponentials1(1, j)
                if first:
                    for m in (WL, WG):
                        for half in range(2):
                            high_weight(m, half)

            steps(act, one)

        @block.gpsimd
        def _(pool):
            nc.gpsimd.memset(ident[:], 0.0).then_inc(eye_cleared, 1)
            pool.wait_ge(eye_cleared, 1)
            nc.gpsimd.affine_select(out=ident[:], in_=ident[:], compare_op=ALU.not_equal, fill=1.0, base=0,
                                    pattern=[[-1, P]], channel_multiplier=1).then_inc(eye_made, 1)
            nc.gpsimd.memset(in_graph[:], 0.0).then_inc(eye_cleared, 1)
            nc.gpsimd.memset(neg_l1[:], NEG_L1).then_inc(const_made, 1)
            nc.gpsimd.memset(minus_half[:], -0.5).then_inc(const_made, 1)
            nc.gpsimd.memset(zero[:], 0.0).then_inc(const_made, 1)
            nc.gpsimd.memset(to_true[:], 1.0 / HN).then_inc(const_made, 1)
            pool.wait_ge(eye_cleared, 2)
            for g in range(2):
                pool.wait_ge(const_made, 4 + g)
                nc.gpsimd.memset(in_graph[N * g:N * g + N, g:g + 1], 1.0).then_inc(const_made, 1)
            pool.wait_ge(const_made, 6)
            nc.gpsimd.memset(p0_place[:], 0.0).then_inc(eye_cleared, 1)
            nc.gpsimd.memset(p1_place[:], 0.0).then_inc(eye_cleared, 1)
            pool.wait_ge(eye_made, 1)
            nc.gpsimd.tensor_tensor(node_eye[:], ident[:, 0:N], ident[:, N:P], ALU.add).then_inc(eye_made, 1)
            pool.wait_ge(const_made, 6)

            def top_weight(m):
                pool.wait_ge(weight_top[m], 2)
                nc.gpsimd.partition_all_reduce(w_all[:, m], w_top[:, m], P, MAX_OVER_PARTITIONS)\
                    .then_inc(weight_all, 1)

            def power(n, g):
                pool.wait_ge(var_ready[n], g + 1)
                nc.gpsimd.tensor_tensor(rstd[n][:], var_eps[n][:], minus_half[:], ALU.pow).then_inc(rstd_ready[n], 1)

            power(0, 0)
            for m in (WQ, WK, WV, WF):
                top_weight(m)
            pool.wait_ge(eye_made, 2)
            pool.wait_ge(const_loaded, 6 * DMA)

            def one(i, now, mid, last, nxt):
                j, p = i - 1, i - 2
                first = isinstance(i, int) and i == 0
                if isinstance(i, int) and i == 1:
                    power(1, j)
                    pool.wait_ge(weight_ready, 12)
                    nc.gpsimd.memset(units(7, 2), 0.0).then_inc(pt1_cleared, 1)
                elif mid:
                    power(1, j)
                tail, final = mid and not now, last and not mid

                def add_bias(t):
                    pool.wait_ge(o_norm, 2 * p + t + 1)
                    o = scratch(t, p)[0].rearrange("p (a n) -> p a n", a=H1)
                    nc.gpsimd.tensor_tensor(o, o, b1_row[:].unsqueeze(1).broadcast_to([P, H1, E1]), ALU.add)\
                        .then_inc(o_biased, 1)

                def add_h(t):
                    pool.wait_ge(summed, 2 * p + t + 1)
                    nc.gpsimd.tensor_tensor(keep[:, t, :], keep[:, t, :], scratch(t, p)[2], ALU.add)\
                        .then_inc(y_ready, 1)

                def keep_copy():
                    after(pool, out_stored, 2 * DMA * j)
                    after(pool, rows1_ready, 2 * j + 2)
                    both = to_true[:].broadcast_to([P, T])
                    nc.gpsimd.tensor_tensor(keep_rstd[:], rstd[1][:], both, ALU.mult)
                    nc.gpsimd.tensor_tensor(keep_shift[:], shift[1][:], both, ALU.mult)
                    nc.gpsimd.tensor_copy(keep, x1).then_inc(kept, 1)

                if final:
                    add_bias(0)
                    add_bias(1)
                    add_h(0)
                    add_h(1)
                elif last:
                    for t in range(T):
                        add_bias(t)
                        add_h(t)
                if mid and not tail:
                    keep_copy()
                if nxt:
                    power(0, i + 1)
                if mid:
                    for t in range(T):
                        pool.wait_ge(th_ready, 2 * j + t + 1)
                        if t == 0:
                            after(pool, summed, 2 * p + 2)
                            if tail:
                                pool.wait_ge(y_ready, 2 * p + 2)
                        else:
                            pool.wait_ge(dst_ready, 2 * j + 1)
                        nc.gpsimd.tensor_tensor(s2, s1, src_row[:], ALU.mult).then_inc(src_prod, 1)
                        nc.gpsimd.tensor_tensor(s3, s1, dst_row[:], ALU.mult).then_inc(dst_prod, 1)
                if now:
                    pool.wait_ge(x1_loaded, DMA * (i + 1))
                    for t in range(T):
                        nc.gpsimd.tensor_tensor(x1[:, t, :], x1[:, t, :], bf_row[:], ALU.add).then_inc(bf_added, 1)
                if mid:
                    pool.wait_ge(parts_ready, j + 1)
                    shape = [P, T, 2, PARTS1]
                    nc.gpsimd.tensor_tensor(
                        dst_terms[:, :, PARTS1:].rearrange("p t (g q) -> p t g q", g=2),
                        parts[:, :, 1, :].unsqueeze(2).broadcast_to(shape),
                        in_graph[:].unsqueeze(1).unsqueeze(3).broadcast_to(shape), ALU.mult)\
                        .then_inc(dst_terms_ready, 1)
                    if tail:
                        keep_copy()
                if first:
                    top_weight(WL)
                    top_weight(WG)

            steps(pool, one)


_INS = ['x', 'adj', 'L0_gnn_Wq', 'L0_gnn_bq', 'L0_gnn_Wk', 'L0_gnn_bk', 'L0_gnn_Wv', 'L0_gnn_bv', 'L0_gnn_Wf',
        'L0_gnn_bf', 'L1_gnn_W', 'L1_gnn_b', 'L1_gnn_w_src', 'L1_gnn_w_dst', 'L1_gnn_H_w', 'L1_gnn_H_b']


def kernel(**inputs):
    import concourse.bacc as bacc
    from concourse.bass_utils import run_bass_kernel_spmd

    arrays = {name: np.ascontiguousarray(inputs[name]) for name in _INS}

    for name in ('L0_gnn_bq', 'L0_gnn_bk'):
        arrays[name] = np.ascontiguousarray(arrays[name].reshape(-1, P).T)
    heads, features, width = arrays['L1_gnn_W'].shape
    arrays['L1_gnn_W'] = np.ascontiguousarray(arrays['L1_gnn_W'].transpose(1, 0, 2).reshape(features, heads * width))
    arrays['L1_gnn_H_w'] = np.ascontiguousarray(arrays['L1_gnn_H_w'].T)

    nc = bacc.Bacc("TRN2", target_bir_lowering=False, num_devices=1)
    args = [nc.dram_tensor(f"in_{n}", arrays[n].shape, mybir.dt.from_np(arrays[n].dtype), kind="ExternalInput").ap()
            for n in _INS]
    out = nc.dram_tensor("out_0", arrays['x'].shape, F32, kind="ExternalOutput").ap()
    build_two_layer_gnn(nc, *args, out)
    r = run_bass_kernel_spmd(nc, [{f"in_{n}": arrays[n] for n in _INS}], core_ids=[0])
    return r.results[0]["out_0"]
```

```python
from contextlib import ExitStack

import concourse.bass as bass
import numpy as np
from concourse import mybir


F32 = mybir.dt.float32
F16 = mybir.dt.float16
BF16 = mybir.dt.bfloat16
U32 = mybir.dt.uint32
U8 = mybir.dt.uint8
ALU = mybir.AluOpType
ACT = mybir.ActivationFunctionType
AX_X = mybir.AxisListType.X
AX_XY = mybir.AxisListType.XY
MAX_OVER_PARTITIONS = bass.bass_isa.ReduceOp.max

P = 128
T = 2
EPS = 1e-5
NEG_L0 = 9.0e15
NEG_L1 = -999.0
ALPHA = 0.2
DMA = 16

HN = 1024.0
W_TOP = 2.0 ** 13
HV = 2.0 ** -19
V_TOP = 2.0 ** 14
P_TOP = 2.0 ** 14
EXPONENT = 0x7F800000
TINY = 2.0 ** -100

WQ, WK, WV, WF, WL, WG = range(6)
BY_LARGEST = (WV, WL)


def after(eng, sem, count):
    if not isinstance(count, int) or count > 0:
        eng.wait_ge(sem, count)


def after_alone(eng, passed, sem, count):
    if isinstance(count, int):
        return after(eng, sem, count)
    count = eng.snap(count)
    eng.wait_ge(passed, 1)
    eng.wait_ge(sem, count)


def build_two_layer_gnn(nc, x, adj, wq, bq, wk, bk, wv, bv, wf, bf, wl, b1, w_src, w_dst, wg, bg, out):
    G, N, C = x.shape
    KT = C // P
    H0, H1 = C // 128, w_src.shape[0]
    E1 = C // H1
    PARTS1 = 3 * H1
    GROUPS = G * N // (P * T)
    INV_SQRT_D = 1.0 / float(np.sqrt(128.0))
    assert 2 * N == P and KT == H0 and E1 == N

    x_g = x.rearrange("(g t b) n c -> g (b n) t c", t=T, b=2)
    out_g = out.rearrange("(g t b) n c -> g (b n) t c", t=T, b=2)
    adj_g = adj.rearrange("(g t b) n m -> g (b n) t m", t=T, b=2)

    with ExitStack() as ctx:
        def sb(name, shape, dt=F32):
            return ctx.enter_context(nc.sbuf_tensor(name, shape, dt))

        def sem(name):
            return ctx.enter_context(nc.semaphore(name))

        pair_att = [ctx.enter_context(nc.psum_tensor(f"pair_att{t}", [P, 1024], F32)) for t in range(2)]
        pair_prj = [ctx.enter_context(nc.psum_tensor(f"pair_prj{t}", [P, 1024], F32)) for t in range(2)]

        w_hi = sb("w_hi", [P, 6, KT, C], F16)
        w_lo = sb("w_lo", [P, 6, KT, C], F16)
        bf_row = sb("bf_row", [P, C])
        bv_row = sb("bv_row", [P, C])
        bg_row = sb("bg_row", [P, C])
        src_row = sb("src_row", [P, C])
        dst_row = sb("dst_row", [P, C])
        b1_row = sb("b1_row", [P, E1])
        bq_col = sb("bq_col", [P, KT])
        bk_col = sb("bk_col", [P, KT])
        ident = sb("ident", [P, P])
        ident_bf = sb("ident_bf", [P, P], BF16)
        in_graph = sb("in_graph", [P, 2])
        node_eye = sb("node_eye", [P, N], BF16)
        of_head = sb("of_head", [P, H1])
        of_graph = sb("of_graph", [P, 2])
        logit_lhs = sb("logit_lhs", [P, T, P], BF16)
        dst_terms = sb("dst_terms", [P, T, 3 * PARTS1], BF16)
        parts = sb("parts", [P, T, 2, PARTS1], BF16)
        rest = sb("rest", [P, T, 2, H1])
        neg_l1 = sb("neg_l1", [P, 1])
        zero = sb("zero", [P, 1])
        to_true = sb("to_true", [P, 1])
        minus_half = sb("minus_half", [P, T])
        w_top = sb("w_top", [P, 6, 2])
        w_all = sb("w_all", [P, 6, 2])
        w_pow = sb("w_pow", [P, 8])
        w_rec = sb("w_rec", [P, 8])
        w_scale = sb("w_scale", [P, 8])
        w_undo = sb("w_undo", [P, 8])
        v_bound = sb("v_bound", [P, 4])
        adj_u8 = sb("adj_u8", [P, T, N], U8)
        not_adj = sb("not_adj", [P, T, N], U8)
        bias0 = sb("bias0", [P, T, N])
        bn_out = [sb(f"bn_out{n}", [P, T, 2, 6]) for n in range(2)]
        mean_var = [sb(f"mean_var{n}", [P, T, 2]) for n in range(2)]
        var_eps = [sb(f"var_eps{n}", [P, T]) for n in range(2)]
        rstd = [sb(f"rstd{n}", [P, T]) for n in range(2)]
        shift = [sb(f"shift{n}", [P, T]) for n in range(2)]
        keep_rstd = sb("keep_rstd", [P, T])
        keep_shift = sb("keep_shift", [P, T])
        max0 = sb("max0", [P, T * H0])
        sum0 = sb("sum0", [P, T * H0])
        rinv0 = sb("rinv0", [P, T * H0])
        src_dst = sb("src_dst", [P, T, 2, H1])
        max1 = sb("max1", [P, T, H1])
        sum1 = sb("sum1", [P, T, H1])
        rinv1 = sb("rinv1", [P, T, H1])

        arena = sb("arena", [P, 23 * C])

        def units(first, n):
            return arena[:, first * C:(first + n) * C]

        def tiles(first):
            return units(first, T).rearrange("p (t c) -> p t c", t=T)

        def split(first, shape, **k):
            v = units(first, 2).bitcast(F16)
            return [v[:, n * 2 * C:(n + 1) * 2 * C].rearrange(shape, **k) for n in range(2)]

        h1v_hi, h1v_lo = split(0, "p (t c) -> p t c", t=T)
        gate = tiles(2)
        s1, s2, s3 = units(4, 1), units(5, 1), units(6, 1)
        pt1_hi, pt1_lo = split(7, "p (a n) -> p a n", a=H1)
        ht1_hi, ht1_lo = split(9, "p (k n) -> p k n", k=KT)
        keep = tiles(11)
        rows = tiles(13)
        x1 = tiles(15)
        ht0_hi, ht0_lo = split(17, "p (k n) -> p k n", k=KT)
        qt = units(19, 2).rearrange("p (k n) -> p k n", k=KT)
        ct_hi, ct_lo = split(19, "p (t k n) -> p t k n", t=T, k=KT)
        kt = units(21, 2).rearrange("p (k n) -> p k n", k=KT)
        pt0_hi, pt0_lo = split(21, "p (a n) -> p a n", a=T * H0)
        p0_place = sb("p0_place", [P, (T * H0 + 2) * N])
        p0 = p0_place[:, N:N + C].rearrange("p (h n) -> p h n", h=T * H0)
        p1_place = sb("p1_place", [P, (T * (H1 + 1) + 1) * N])
        p1 = p1_place[:, N:].rearrange("p (t a n) -> p t a n", t=T, a=H1 + 1)[:, :, 0:H1, :]
        vals_hi, vals_lo = [p1_place[:, n * C:(n + 1) * C].bitcast(F16).rearrange("p (t c) -> p t c", t=T)
                            for n in range(2)]
        vals = tiles(19)
        late_hi, late_lo = [w[:, WL:WG + 1].rearrange("p m k n -> p (m k n)").bitcast(F32) for w in (w_hi, w_lo)]

        def is_late(t, g):
            return isinstance(g, int) and g >= GROUPS - 2 and t == T - 1

        def scratch(t, g):
            return (units(17, 1), units(18, 1), units(19, 1)) if is_late(t, g) else (s1, s2, s3)

        def tanh_scratch(t, g):
            if isinstance(g, int) and g == GROUPS - 1:
                return ((units(20, 1), units(13, 1), units(14, 1)), (units(21, 1), units(22, 1), s3))[t]
            return s1, s2, s3

        logit_rhs = [s.bitcast(BF16)[0:3 * PARTS1, 0:C] for s in (s2, s3)]
        staging = [s.rearrange("p (k n) -> p k n", k=KT)
                   for s in (units(0, 6), units(6, 6), late_hi, late_lo, units(0, 6), units(6, 6))]

        const_loaded = sem("const_loaded")
        columns_loaded = sem("columns_loaded")
        weight_loaded = [[sem(f"weight_loaded{m}_{half}") for half in range(2)] for m in range(6)]
        const_made = sem("const_made")
        eye_cleared = sem("eye_cleared")
        eye_made = sem("eye_made")
        rows_marked = sem("rows_marked")
        weight_top = [sem(f"weight_top{m}") for m in range(6)]
        weight_all = sem("weight_all")
        scale_step = sem("scale_step")
        weight_scaled = sem("weight_scaled")
        weight_hi = sem("weight_hi")
        weight_ready = sem("weight_ready")
        wf_scaled = sem("wf_scaled")
        wf_ready = sem("wf_ready")
        rows_loaded = sem("rows_loaded")
        x1_loaded = sem("x1_loaded")
        adj_loaded = sem("adj_loaded")
        out_stored = sem("out_stored")
        bias0_made = sem("bias0_made")
        not_adj_made = sem("not_adj_made")
        bn_done = [sem(f"bn_done{n}") for n in range(2)]
        mean_done = [sem(f"mean_done{n}") for n in range(2)]
        var_ready = [sem(f"var_ready{n}") for n in range(2)]
        rstd_ready = [sem(f"rstd_ready{n}") for n in range(2)]
        shift_ready = [sem(f"shift_ready{n}") for n in range(2)]
        rows0_ready = sem("rows0_ready")
        rows1_ready = sem("rows1_ready")
        t0_psum = sem("t0_psum")
        ht0_hi_ready = sem("ht0_hi_ready")
        ht0_ready = sem("ht0_ready")
        t1_psum = sem("t1_psum")
        ht1_hi_ready = sem("ht1_hi_ready")
        ht1_ready = sem("ht1_ready")
        q_psum = sem("q_psum")
        q_ready = sem("q_ready")
        k_psum = sem("k_psum")
        k_ready = sem("k_ready")
        v_psum = sem("v_psum")
        v_read = sem("v_read")
        v_hi_ready = sem("v_hi_ready")
        v_ready = sem("v_ready")
        s_psum = sem("s_psum")
        s_ready = sem("s_ready")
        max0_ready = sem("max0_ready")
        shifted0 = sem("shifted0")
        exp0_ready = sem("exp0_ready")
        sum0_ready = sem("sum0_ready")
        rinv0_ready = sem("rinv0_ready")
        p0_ready = sem("p0_ready")
        pt0_cleared = sem("pt0_cleared")
        pt0_psum = sem("pt0_psum")
        pt0_hi_ready = sem("pt0_hi_ready")
        pt0_ready = sem("pt0_ready")
        ct_psum = sem("ct_psum")
        ct_hi_ready = sem("ct_hi_ready")
        ct_ready = sem("ct_ready")
        f_psum = sem("f_psum")
        bf_added = sem("bf_added")
        x1_ready = sem("x1_ready")
        kept = sem("kept")
        h_psum = sem("h_psum")
        th_ready = sem("th_ready")
        h_ready = sem("h_ready")
        src_prod = sem("src_prod")
        dst_prod = sem("dst_prod")
        src_ready = sem("src_ready")
        dst_ready = sem("dst_ready")
        part1_ready = sem("part1_ready")
        rest_ready = sem("rest_ready")
        part2_ready = sem("part2_ready")
        parts_ready = sem("parts_ready")
        dst_terms_ready = sem("dst_terms_ready")
        lhs_psum = sem("lhs_psum")
        rhs_psum = sem("rhs_psum")
        logit_lhs_ready = sem("logit_lhs_ready")
        logit_rhs_ready = sem("logit_rhs_ready")
        g_psum = sem("g_psum")
        g_ready = sem("g_ready")
        gate_ready = sem("gate_ready")
        z_psum = sem("z_psum")
        z_ready = sem("z_ready")
        leaky_ready = sem("leaky_ready")
        masked1 = sem("masked1")
        max1_ready = sem("max1_ready")
        shifted1 = sem("shifted1")
        exp1_ready = sem("exp1_ready")
        sum1_ready = sem("sum1_ready")
        rinv1_ready = sem("rinv1_ready")
        rinv1_scaled = sem("rinv1_scaled")
        pt1_cleared = sem("pt1_cleared")
        pt1_psum = sem("pt1_psum")
        pt1_hi_ready = sem("pt1_hi_ready")
        pt1_ready = sem("pt1_ready")
        o_psum = sem("o_psum")
        o_norm = sem("o_norm")
        o_biased = sem("o_biased")
        o_min = sem("o_min")
        h_again = sem("h_again")
        o_exp = sem("o_exp")
        elu_ready = sem("elu_ready")
        diff_ready = sem("diff_ready")
        gated = sem("gated")
        summed = sem("summed")
        y_ready = sem("y_ready")

        block = ctx.enter_context(nc.Block())

        def columns(half):
            return slice(half * (C // 2), (half + 1) * (C // 2))

        WINDOWS = ((0, 7), (7, 13))

        def heads_in(half, g):
            return (slice(0, 6), slice(0, 7))[g] if half == 0 else (slice(6, 12), slice(7, 12))[g]

        def diagonal(pair, half, g):
            v = pair.rearrange("p (w n) -> p w n", n=P)
            windows = (slice(1, 7), slice(0, 7))[g] if half == 0 else (slice(0, 6), slice(0, 5))[g]
            return v[N * g:N * g + N, windows, N * g:N * g + N]

        def steps(eng, one):
            def flags(i):
                return [0 <= g < GROUPS for g in (i, i - 1, i - 2, i + 1)]
            for i in (0, 1):
                one(i, *flags(i))
            with eng.Fori(2, GROUPS - 1) as i:
                one(i, True, True, True, True)
            for i in range(GROUPS - 1, GROUPS + 2):
                one(i, *flags(i))

        @block.sync
        def _(sp):
            weights = [wq, wk, wv, wf, wl, wg]

            def load_weight(m):
                w = weights[m].rearrange("(k p) n -> p k n", p=P)
                for half in range(2):
                    sp.dma_start(staging[m][:, :, columns(half)], w[:, :, columns(half)])\
                        .then_inc(weight_loaded[m][half], DMA)

            sp.dma_start(rows, x_g[0]).then_inc(rows_loaded, DMA)
            load_weight(WQ)
            for dst, src in ((bq_col, bq), (bk_col, bk)):
                sp.dma_start(dst[:], src).then_inc(columns_loaded, DMA)
            load_weight(WK)
            load_weight(WV)
            sp.dma_start(x1, x_g[0]).then_inc(x1_loaded, DMA)
            for dst, src in ((bf_row, bf), (bv_row, bv), (bg_row, bg), (b1_row, b1)):
                sp.dma_start(dst[:], src.partition_broadcast(P)).then_inc(const_loaded, DMA)
            for dst, src in ((src_row, w_src), (dst_row, w_dst)):
                sp.dma_start(dst[:], src.rearrange("a e o -> (a e o)").partition_broadcast(P)).then_inc(const_loaded, DMA)
            load_weight(WF)
            sp.dma_start(adj_u8[:], adj_g[0]).then_inc(adj_loaded, DMA)
            sp.wait_ge(t0_psum, 2)
            sp.dma_start(rows, x_g[1]).then_inc(rows_loaded, DMA)
            sp.wait_ge(weight_ready, 2 * (WQ + 1))
            load_weight(WL)
            sp.wait_ge(weight_ready, 2 * (WK + 1))
            load_weight(WG)

            def one(i, now, mid, last, nxt):
                j, p = i - 1, i - 2
                first = isinstance(i, int) and i == 0
                if now and not first:
                    after_alone(sp, eye_made, not_adj_made, i)
                    sp.dma_start(adj_u8[:], adj_g[i]).then_inc(adj_loaded, DMA)
                if last:
                    after_alone(sp, eye_made, y_ready, 2 * p + 1)
                    sp.dma_start(out_g[p, :, 0, :], keep[:, 0, :]).then_inc(out_stored, DMA)
                if nxt and not first:
                    after_alone(sp, eye_made, t0_psum, 2 * i + 2)
                    if mid:
                        after_alone(sp, eye_made, t1_psum, 2 * j + 2)
                    sp.dma_start(rows, x_g[i + 1]).then_inc(rows_loaded, DMA)
                if last:
                    after_alone(sp, eye_made, y_ready, 2 * p + 2)
                    sp.dma_start(out_g[p, :, 1, :], keep[:, 1, :]).then_inc(out_stored, DMA)
                if now and mid:
                    after_alone(sp, eye_made, rows1_ready, 2 * j + 2)
                    after_alone(sp, eye_made, kept, j + 1)
                    sp.dma_start(x1, x_g[i]).then_inc(x1_loaded, DMA)

            steps(sp, one)
            sp.wait_ge(out_stored, 2 * DMA * GROUPS)

        @block.tensor
        def _(pe):
            def weight(m, k, part):
                return (w_hi, w_lo)[part][:, m, k, :]

            def project_rows(m, lhs, t, pair, done):
                for lo, hi in ((0, 512), (512, C)):
                    for k in range(KT):
                        for n, (a, b) in enumerate(((0, 0), (0, 1), (1, 0))):
                            mm = nc.tensor.matmul(pair[:, lo:hi], lhs(a, k), weight(m, k, b)[:, lo:hi],
                                                  start=(k == 0 and n == 0), stop=(k == KT - 1 and n == 2))
                mm.then_inc(done, 1)

            def project_columns(m, half, pair, done):
                for c in range(3):
                    o = (3 * half + c) * P
                    for k in range(KT):
                        for n, (a, b) in enumerate(((0, 0), (0, 1), (1, 0))):
                            mm = nc.tensor.matmul(pair[:, c * 256:(c + 1) * 256], weight(m, k, a)[:, o:o + P],
                                                  (ht0_hi, ht0_lo)[b][:, k, :],
                                                  start=(k == 0 and n == 0), stop=(k == KT - 1 and n == 2))
                mm.then_inc(done, 1)

            def transpose_rows(t, done):
                for k in range(KT):
                    mm = nc.tensor.transpose(pair_prj[t][:, k * P:(k + 1) * P], rows[:, t, k * P:(k + 1) * P], ident[:])
                mm.then_inc(done, 1)

            def transpose_windows(half, place, block, done, psum=pair_att):
                for n, w in enumerate(range(*WINDOWS[half])):
                    c = (block + w) * N
                    mm = nc.tensor.transpose(psum[half][:, n * P:(n + 1) * P], place[:, c:c + 2 * N], ident[:])
                mm.then_inc(done, 1)

            def transpose_p1(t, half, psum=pair_att):
                transpose_windows(half, p1_place, t * (H1 + 1), pt1_psum, psum)

            def attend1(t):
                for a in range(H1):
                    c = slice(a * E1, (a + 1) * E1)
                    parts = ((pt1_hi, h1v_hi), (pt1_hi, h1v_lo), (pt1_lo, h1v_hi))
                    for n, (pt, hv) in enumerate(parts):
                        mm = nc.tensor.matmul(pair_att[t][:, c], pt[:, a, :], hv[:, t, c], start=(n == 0), stop=(n == 2))
                mm.then_inc(o_psum, 1)

            pe.wait_ge(eye_made, 2)
            for t in range(T):
                pe.wait_ge(rows0_ready, t + 1)
                transpose_rows(t, t0_psum)

            def one(i, now, mid, last, nxt):
                j, p = i - 1, i - 2
                first = isinstance(i, int) and i == 0
                first_mid = isinstance(i, int) and i == 1
                tail, final = mid and not now, last and not mid

                def project_h(t):
                    pe.wait_ge(ht1_ready, 2 * j + t + 1)
                    if now:
                        pe.wait_ge(v_read, 2 * i + t + 1)
                    project_rows(WL, lambda a, k: (ht1_hi, ht1_lo)[a][:, k, t * P:(t + 1) * P], t,
                                 pair_prj[t], h_psum)

                if now:
                    if first:
                        pe.wait_ge(weight_ready, 2 * WQ + 1)
                    pe.wait_ge(ht0_ready, 2 * i + 2)
                    after(pe, x1_ready, 2 * i - 1)
                    project_columns(WQ, 0, pair_prj[0], q_psum)
                if last:
                    pe.wait_ge(exp1_ready, 2 * p + 1)
                    transpose_p1(0, 0)
                    pe.wait_ge(z_ready, 2 * p + 2)
                    transpose_p1(0, 1)
                if now:
                    if first:
                        pe.wait_ge(weight_ready, 2 * WQ + 2)
                    after(pe, x1_ready, 2 * i)
                    project_columns(WQ, 1, pair_prj[1], q_psum)
                if tail:
                    for t in range(T):
                        pe.wait_ge(rows1_ready, 2 * j + t + 1)
                        transpose_rows(t, t1_psum)
                if last:
                    pe.wait_ge(h_ready, 2 * p + 2)
                    pe.wait_ge(pt1_ready, 4 * p + 2)
                    attend1(0)
                if now:
                    if first:
                        pe.wait_ge(weight_ready, 2 * WK + 1)
                    pe.wait_ge(q_ready, 2 * i + 1)
                    project_columns(WK, 0, pair_prj[0], k_psum)
                if final:
                    pe.wait_ge(exp1_ready, 2 * p + 2)
                    transpose_p1(1, 0, pair_prj)
                    transpose_p1(1, 1, pair_prj)
                elif last:
                    pe.wait_ge(exp1_ready, 2 * p + 2)
                    pe.wait_ge(o_norm, 2 * p + 1)
                    transpose_p1(1, 0)
                    transpose_p1(1, 1)
                if now:
                    if first:
                        pe.wait_ge(weight_ready, 2 * WK + 2)
                    pe.wait_ge(q_ready, 2 * i + 2)
                    project_columns(WK, 1, pair_prj[1], k_psum)
                if tail:
                    project_h(0)
                if last:
                    pe.wait_ge(pt1_ready, 4 * p + 4)
                    attend1(1)

                if mid and not tail:
                    for t in range(T):
                        pe.wait_ge(rows1_ready, 2 * j + t + 1)
                        if now:
                            pe.wait_ge(k_ready, 2 * i + t + 1)
                        transpose_rows(t, t1_psum)

                if now:
                    pe.wait_ge(k_ready, 2 * i + 2)
                    for t in range(T):
                        if last and t == 0:
                            pe.wait_ge(pt1_ready, 4 * p + 3)
                        elif last:
                            pe.wait_ge(o_norm, 2 * p + 2)
                        else:
                            after(pe, ct_ready, 2 * i - 1 + t)
                        for h in range(H0):
                            mm = nc.tensor.matmul(pair_att[t][:, h * P:(h + 1) * P], qt[:, h, t * P:(t + 1) * P],
                                                  kt[:, h, t * P:(t + 1) * P], start=True, stop=True)
                        mm.then_inc(s_psum, 1)

                    if first:
                        pe.wait_ge(weight_ready, 2 * WV + 2)
                    for t in range(T):
                        if mid:
                            pe.wait_ge(ht1_ready, 2 * j + t + 1)
                        else:
                            pe.wait_ge(k_ready, 2 * i + t + 1)
                        project_rows(WV, lambda a, k: (ht0_hi, ht0_lo)[a][:, k, t * P:(t + 1) * P], t,
                                     pair_prj[t], v_psum)

                if mid:
                    if first_mid:
                        pe.wait_ge(weight_ready, 2 * WL)
                    if not tail:
                        project_h(0)
                if now:
                    pe.wait_ge(p0_ready, i + 1)
                    for t in range(T):
                        transpose_windows(t, p0_place, 0, pt0_psum)
                if mid:
                    project_h(1)

                def next_rows(t):
                    if nxt:
                        pe.wait_ge(rows0_ready, 2 * i + t + 3)
                        if mid:
                            pe.wait_ge(h_ready, 2 * j + t + 1)
                        else:
                            pe.wait_ge(v_read, 2 * i + t + 1)
                        transpose_rows(t, t0_psum)

                def context(t):
                    if now:
                        pe.wait_ge(v_ready, 2 * i + t + 1)
                        pe.wait_ge(pt0_ready, 2 * i + t + 1)
                        parts0 = ((vals_hi, pt0_hi), (vals_hi, pt0_lo), (vals_lo, pt0_hi))
                        for h in range(H0):
                            for n, (v, pt) in enumerate(parts0):
                                mm = nc.tensor.matmul(pair_att[t][:, h * P:(h + 1) * P], v[:, t, h * P:(h + 1) * P],
                                                      pt[:, t * H0 + h, :], start=(n == 0), stop=(n == 2))
                        mm.then_inc(ct_psum, 1)

                next_rows(0)
                context(0)
                context(1)
                next_rows(1)

                def logit_operands():
                    pe.wait_ge(dst_terms_ready, j + 1)
                    for t in range(T):
                        if now:
                            pe.wait_ge(ct_ready, 2 * i + t + 1)
                        elif last and t == 0:
                            pe.wait_ge(pt1_ready, 4 * p + 3)
                        elif last:
                            pe.wait_ge(o_norm, 2 * p + 2)
                        nc.tensor.matmul(pair_att[t][0:PARTS1, 0:P], parts[:, t, 0, :], ident_bf[:],
                                         start=True, stop=True).then_inc(lhs_psum, 1)
                        nc.tensor.matmul(pair_att[t][0:3 * PARTS1, 512:512 + N], dst_terms[:, t, :], node_eye[:],
                                         start=True, stop=True).then_inc(rhs_psum, 1)

                if mid:
                    if first_mid:
                        pe.wait_ge(weight_ready, 2 * WG)
                        pe.wait_ge(rows_marked, 4 + T)
                    for t in range(T):
                        if nxt:
                            pe.wait_ge(ht0_ready, 2 * i + t + 3)
                        else:
                            pe.wait_ge(h_ready, 2 * j + t + 1)
                        project_rows(WG, lambda a, k: (ht1_hi, ht1_lo)[a][:, k, t * P:(t + 1) * P], t,
                                     pair_prj[t], g_psum)
                        if t == (1 if tail else 0):
                            logit_operands()

                    for t in range(T):
                        pe.wait_ge(logit_lhs_ready, 2 * j + t + 1)
                        pe.wait_ge(logit_rhs_ready, 2 * j + t + 1)
                        for lo, hi in ((0, 512), (512, C)):
                            mm = nc.tensor.matmul(pair_att[t][:, lo:hi], logit_lhs[0:3 * PARTS1, t, :],
                                                  logit_rhs[t][:, lo:hi], start=True, stop=True)
                        mm.then_inc(z_psum, 1)

                if now:
                    if first:
                        pe.wait_ge(wf_ready, 2)
                    for t in range(T):
                        pe.wait_ge(ct_ready, 2 * i + t + 1)
                        if mid:
                            pe.wait_ge(g_ready, 2 * j + t + 1)
                        else:
                            pe.wait_ge(ht0_ready, 2 * i + t + 3)
                        project_rows(WF, lambda a, k: (ct_hi, ct_lo)[a][:, t, k, :], t, pair_prj[t], f_psum)

            steps(pe, one)

        @block.vector
        def _(dve):
            made = [0]

            def scale(ins):
                made[0] += 1
                ins.then_inc(scale_step, 1)
                dve.wait_ge(scale_step, made[0])

            def col(tensor, n):
                return tensor[:, n:n + 1]

            def power_of_two(dst, src):
                scale(nc.vector.tensor_scalar(dst.bitcast(U32), src.bitcast(U32), EXPONENT, None, ALU.bitwise_and))
                scale(nc.vector.tensor_scalar(dst, dst, TINY, None, ALU.max))

            def largest(m, half):
                dve.wait_ge(weight_loaded[m][half], DMA)
                nc.vector.tensor_reduce(w_top[:, m, half:half + 1], staging[m][:, :, columns(half)], AX_XY, ALU.max,
                                        apply_absolute_value=True).then_inc(weight_top[m], 1)

            def scale_weight(m):
                dve.wait_ge(weight_all, m + 1)
                scale(nc.vector.tensor_tensor(col(w_pow, m), w_all[:, m, 0:1], w_all[:, m, 1:2],
                                              ALU.max if m in BY_LARGEST else ALU.add))
                power_of_two(col(w_pow, m), col(w_pow, m))
                scale(nc.vector.reciprocal(col(w_rec, m), col(w_pow, m)))
                nc.vector.tensor_scalar(col(w_scale, m), col(w_rec, m), W_TOP, None, ALU.mult).then_inc(weight_scaled, 1)
                undo = 1.0 / W_TOP if m == WF else 1.0 / (W_TOP * HN)
                scale(nc.vector.tensor_scalar(col(w_undo, m), col(w_pow, m), undo, None, ALU.mult))
                if m == WV:
                    dve.wait_ge(const_loaded, 6 * DMA)
                    scale(nc.vector.tensor_reduce(col(w_pow, 6), bv_row[:], AX_X, ALU.max, apply_absolute_value=True))
                    power_of_two(col(w_pow, 6), col(w_pow, 6))
                    scale(nc.vector.tensor_scalar(col(v_bound, 0), col(w_pow, 6), 2.0, None, ALU.mult))
                    scale(nc.vector.scalar_tensor_tensor(col(v_bound, 0), col(w_pow, WV), 2048.0, col(v_bound, 0),
                                                         ALU.mult, ALU.add))
                    power_of_two(col(v_bound, 1), col(v_bound, 0))
                    scale(nc.vector.reciprocal(col(v_bound, 2), col(v_bound, 1)))
                    scale(nc.vector.tensor_scalar(col(v_bound, 2), col(v_bound, 2), V_TOP, None, ALU.mult))
                    scale(nc.vector.tensor_scalar(bv_row[:], bv_row[:], col(v_bound, 2), None, ALU.mult))
                    scale(nc.vector.tensor_tensor(col(w_undo, WV), col(w_undo, WV), col(v_bound, 2), ALU.mult))
                if m == WF:
                    scale(nc.vector.tensor_scalar(col(v_bound, 3), col(v_bound, 1), 1.0 / V_TOP, None, ALU.mult))
                    scale(nc.vector.tensor_tensor(col(w_undo, WF), col(w_undo, WF), col(v_bound, 3), ALU.mult))
                if m == WL:
                    scale(nc.vector.tensor_scalar(col(w_undo, 7), col(w_undo, WL), 1.0 / (HV * P_TOP), None, ALU.mult))

            def low_weight(m, half):
                dve.wait_ge(weight_hi, 2 * m + half + 1)
                nc.vector.scalar_tensor_tensor(w_lo[:, m, :, columns(half)], staging[m][:, :, columns(half)],
                                               col(w_scale, m), w_hi[:, m, :, columns(half)],
                                               ALU.mult, ALU.subtract).then_inc(weight_ready, 1)

            def moments(n, src, t):
                for c in range(2):
                    bn = nc.vector.bn_stats(bn_out[n][:, t, c, :], src[:, t, c * (C // 2):(c + 1) * (C // 2)])
                if t == T - 1:
                    bn.then_inc(bn_done[n], 1)

            def statistics(n, src, g, begun=False):
                for t in range(T):
                    if not begun:
                        moments(n, src, t)
                after_alone(dve, eye_made, bn_done[n], g + 1)
                for t in range(T):
                    ag = nc.vector.bn_aggr(mean_var[n][:, t, :], bn_out[n][:, t].rearrange("p c s -> p (c s)"))
                ag.then_inc(mean_done[n], 1)
                dve.wait_ge(mean_done[n], g + 1)
                nc.vector.tensor_scalar(var_eps[n][:], mean_var[n][:, :, 1], EPS, 1.0 / (HN * HN), ALU.add, ALU.mult)\
                    .then_inc(var_ready[n], 1)
                dve.wait_ge(rstd_ready[n], g + 1)
                nc.vector.scalar_tensor_tensor(shift[n][:], mean_var[n][:, :, 0], -1.0, rstd[n][:],
                                               ALU.mult, ALU.mult).then_inc(shift_ready[n], 1)

            def low_part_transposed(t, g, hi_t, lo_t, hi_ready, ready):
                dve.wait_ge(hi_ready, 2 * g + t + 1)
                nc.vector.tensor_tensor(lo_t[:, :, t * P:(t + 1) * P],
                                        pair_prj[t][:, 0:C].rearrange("p (k n) -> p k n", k=KT),
                                        hi_t[:, :, t * P:(t + 1) * P], ALU.subtract).then_inc(ready, 1)

            def biased_columns(half, pair, dst, bias, m, ready):
                nc.vector.scalar_tensor_tensor(
                    dst[:, 3 * half:3 * half + 3, :], pair[:, 0:C].rearrange("p (c n) -> p c n", c=3), col(w_undo, m),
                    bias[:, 3 * half:3 * half + 3].unsqueeze(2).broadcast_to([P, 3, 2 * P]),
                    ALU.mult, ALU.add).then_inc(ready, 1)

            def pt1_low(t, half, p, psum=pair_att):
                dve.wait_ge(pt1_hi_ready, 4 * p + 2 * t + half + 1)
                for g in range(2):
                    r = slice(N * g, N * g + N)
                    heads = heads_in(half, g)
                    lo = nc.vector.scalar_tensor_tensor(pt1_lo[r, heads, r], diagonal(psum[half][:], half, g), P_TOP,
                                                        pt1_hi[r, heads, r], ALU.mult, ALU.subtract)
                lo.then_inc(pt1_ready, 1)

            def sum_and_invert(t, g):
                n = 2 * g + t + 1
                dve.wait_ge(exp1_ready, n)
                nc.vector.tensor_reduce(sum1[:, t, :], p1[:, t], AX_X, ALU.add).then_inc(sum1_ready, 1)
                dve.wait_ge(sum1_ready, n)
                nc.vector.reciprocal(rinv1[:, t, :], sum1[:, t, :]).then_inc(rinv1_ready, 1)
                dve.wait_ge(rinv1_ready, n)
                nc.vector.tensor_scalar(rinv1[:, t, :], rinv1[:, t, :], col(w_undo, 7), None, ALU.mult)\
                    .then_inc(rinv1_scaled, 1)

            def heads1(ap):
                return ap.rearrange("p (a n) -> p a n", a=H1)

            def output_first(t, p):
                s1, s2, s3 = scratch(t, p)
                dve.wait_ge(rinv1_scaled, 2 * p + t + 1)
                dve.wait_ge(o_psum, 2 * p + t + 1)
                nc.vector.tensor_tensor(heads1(s1), heads1(pair_att[t][:, 0:C]),
                                        rinv1[:, t, :].unsqueeze(2).broadcast_to([P, H1, E1]), ALU.mult)\
                    .then_inc(o_norm, 1)

            def output_min(t, p):
                s1, s2, s3 = scratch(t, p)
                dve.wait_ge(o_biased, 2 * p + t + 1)
                nc.vector.tensor_scalar(s2, s1, 0.0, None, ALU.min).then_inc(o_min, 1)

            def output_last(t, p):
                s1, s2, s3 = scratch(t, p)
                n = 2 * p + t + 1
                dve.wait_ge(o_exp, n)
                nc.vector.scalar_tensor_tensor(s1, s2, -1.0, s1, ALU.add, ALU.max).then_inc(elu_ready, 1)
                dve.wait_ge(elu_ready, n)
                dve.wait_ge(h_again, n)
                nc.vector.tensor_tensor(s2, s1, s3, ALU.subtract).then_inc(diff_ready, 1)
                dve.wait_ge(diff_ready, n)
                dve.wait_ge(gate_ready, n)
                nc.vector.scalar_tensor_tensor(s2, gate[:, t, :], 1.0, s2, ALU.add, ALU.mult).then_inc(gated, 1)
                dve.wait_ge(gated, n)
                nc.vector.scalar_tensor_tensor(keep[:, t, :], s2, 0.5, keep[:, t, :], ALU.mult, ALU.add)\
                    .then_inc(summed, 1)

            dve.wait_ge(eye_made, 1)
            nc.vector.tensor_copy(ident_bf[:], ident[:]).then_inc(rows_marked, 1)
            nc.vector.tensor_reduce(of_head[:], ident[:, 0:3 * PARTS1].rearrange("p (q a) -> p a q", a=H1), AX_X,
                                    ALU.add).then_inc(rows_marked, 1)
            nc.vector.tensor_reduce(of_graph[:], ident[:, PARTS1:3 * PARTS1].rearrange("p (g q) -> p g q", g=2), AX_X,
                                    ALU.add).then_inc(rows_marked, 1)
            for t in range(T):
                nc.vector.tensor_scalar(dst_terms[:, t, :], ident[:, 0:3 * PARTS1], 0.0, 0.5, ALU.mult, ALU.add)\
                    .then_inc(rows_marked, 1)
            dve.wait_ge(rows_marked, 3 + T)
            nc.vector.tensor_copy(logit_lhs[:].rearrange("p t (g n) -> p t g n", g=2),
                                  of_graph[:].unsqueeze(1).unsqueeze(3).broadcast_to([P, T, 2, N]))\
                .then_inc(rows_marked, 1)
            dve.wait_ge(eye_cleared, 4)
            dve.wait_ge(rows_loaded, DMA)
            statistics(0, rows, 0)
            largest(WQ, 1)
            scale_weight(WQ)
            for t in range(T):
                low_part_transposed(t, 0, ht0_hi, ht0_lo, ht0_hi_ready, ht0_ready)
            low_weight(WQ, 0)
            low_weight(WQ, 1)
            largest(WV, 0)
            scale_weight(WK)
            largest(WV, 1)
            low_weight(WK, 0)
            dve.wait_ge(columns_loaded, 2 * DMA)

            def one(i, now, mid, last, nxt):
                j, p = i - 1, i - 2
                first = isinstance(i, int) and i == 0
                tail, final = mid and not now, last and not mid
                def h_low(t):
                    dve.wait_ge(th_ready, 2 * j + t + 1)
                    nc.vector.scalar_tensor_tensor(h1v_lo[:, t, :], pair_prj[t][:, 0:C], HV, h1v_hi[:, t, :],
                                                   ALU.mult, ALU.subtract).then_inc(h_ready, 1)

                def source_and_target(t):
                    dve.wait_ge(src_prod, 2 * j + t + 1)
                    nc.vector.tensor_reduce(src_dst[:, t, 0, :], heads1(tanh_scratch(t, j)[1]), AX_X, ALU.add).then_inc(src_ready, 1)
                    dve.wait_ge(dst_prod, 2 * j + t + 1)
                    nc.vector.tensor_reduce(src_dst[:, t, 1, :], heads1(tanh_scratch(t, j)[2]), AX_X, ALU.add).then_inc(dst_ready, 1)

                if mid and not tail:
                    dve.wait_ge(x1_ready, 2 * j + 2)
                    statistics(1, x1, j)
                if now:
                    dve.wait_ge(q_psum, 2 * i + 1)
                    biased_columns(0, pair_prj[0], qt, bq_col, WQ, q_ready)
                if isinstance(i, int) and i == 1:
                    for half in range(2):
                        low_weight(WG, half)
                if first:
                    low_weight(WK, 1)
                    scale_weight(WV)
                if last:
                    pt1_low(0, 0, p)
                    pt1_low(0, 1, p)
                if now:
                    dve.wait_ge(q_psum, 2 * i + 2)
                    biased_columns(1, pair_prj[1], qt, bq_col, WQ, q_ready)
                if first:
                    low_weight(WV, 0)
                if tail:
                    low_part_transposed(0, j, ht1_hi, ht1_lo, ht1_hi_ready, ht1_ready)
                    low_part_transposed(1, j, ht1_hi, ht1_lo, ht1_hi_ready, ht1_ready)
                if final:
                    sum_and_invert(1, p)
                if last:
                    output_first(0, p)
                if final:
                    pt1_low(1, 0, p, pair_prj)
                    pt1_low(1, 1, p, pair_prj)
                if last:
                    output_min(0, p)
                if now:
                    dve.wait_ge(k_psum, 2 * i + 1)
                    biased_columns(0, pair_prj[0], kt, bk_col, WK, k_ready)
                if tail:
                    pt1_low(1, 0, p)
                    pt1_low(1, 1, p)
                if final:
                    output_first(1, p)
                if last:
                    output_last(0, p)
                if last and now:
                    pt1_low(1, 0, p)
                    pt1_low(1, 1, p)
                if now:
                    dve.wait_ge(k_psum, 2 * i + 2)
                    biased_columns(1, pair_prj[1], kt, bk_col, WK, k_ready)
                if first:
                    low_weight(WV, 1)
                    scale_weight(WF)
                if tail:
                    h_low(0)
                if last and not final:
                    output_first(1, p)
                if mid and not tail:
                    low_part_transposed(0, j, ht1_hi, ht1_lo, ht1_hi_ready, ht1_ready)
                if last:
                    output_min(1, p)
                if mid and not tail:
                    low_part_transposed(1, j, ht1_hi, ht1_lo, ht1_hi_ready, ht1_ready)
                if tail:
                    source_and_target(0)
                    h_low(1)
                if last:
                    output_last(1, p)

                if first:
                    dve.wait_ge(rows_loaded, DMA * (i + 2))
                    statistics(0, rows, i + 1)
                if now:
                    dve.wait_ge(adj_loaded, DMA * (i + 1))
                    nc.vector.tensor_scalar(bias0[:], adj_u8[:], -1.0, NEG_L0, ALU.add, ALU.mult).then_inc(bias0_made, 1)
                    dve.wait_ge(bias0_made, i + 1)
                    for t in range(T):
                        dve.wait_ge(s_psum, 2 * i + t + 1)
                        for g in range(2):
                            r = slice(N * g, N * g + N)
                            sc = nc.vector.scalar_tensor_tensor(
                                p0[r, t * H0:(t + 1) * H0, :],
                                pair_att[t][r, 0:C].rearrange("p (h n) -> p h n", h=H0)[:, :, r], INV_SQRT_D,
                                bias0[r, t, :].unsqueeze(1).broadcast_to([N, H0, N]), ALU.mult, ALU.add)
                        sc.then_inc(s_ready, 1)
                    wide = [P, T * H0, N]
                    dve.wait_ge(s_ready, 2 * i + 2)
                    nc.vector.tensor_reduce(max0[:], p0, AX_X, ALU.max).then_inc(max0_ready, 1)
                    dve.wait_ge(max0_ready, i + 1)
                    nc.vector.tensor_tensor(p0, p0, max0[:].unsqueeze(2).broadcast_to(wide), ALU.subtract)\
                        .then_inc(shifted0, 1)

                    def read_values(t):
                        dve.wait_ge(v_psum, 2 * i + t + 1)
                        nc.vector.scalar_tensor_tensor(vals[:, t, :], pair_prj[t][:, 0:C], col(w_undo, WV), bv_row[:],
                                                       ALU.mult, ALU.add).then_inc(v_read, 1)

                    def low_values(t):
                        dve.wait_ge(v_hi_ready, 2 * i + t + 1)
                        nc.vector.tensor_tensor(vals_lo[:, t, :], vals[:, t, :], vals_hi[:, t, :], ALU.subtract)\
                            .then_inc(v_ready, 1)

                    read_values(0)
                    dve.wait_ge(exp0_ready, i + 1)
                    nc.vector.tensor_reduce(sum0[:], p0, AX_X, ALU.add).then_inc(sum0_ready, 1)
                    dve.wait_ge(sum0_ready, i + 1)
                    nc.vector.reciprocal(rinv0[:], sum0[:]).then_inc(rinv0_ready, 1)
                    dve.wait_ge(rinv0_ready, i + 1)
                    nc.vector.tensor_tensor(p0, p0, rinv0[:].unsqueeze(2).broadcast_to(wide), ALU.mult)\
                        .then_inc(p0_ready, 1)
                    low_values(0)
                    read_values(1)
                    low_values(1)
                if nxt and not first:
                    dve.wait_ge(rows_loaded, DMA * (i + 2))
                    statistics(0, rows, i + 1)

                if mid and not tail:
                    h_low(0)
                if now:
                    for t in range(T):
                        dve.wait_ge(pt0_hi_ready, 2 * i + t + 1)
                        for g in range(2):
                            r = slice(N * g, N * g + N)
                            heads = heads_in(t, g)
                            lo = nc.vector.scalar_tensor_tensor(
                                pt0_lo[r, heads, r], diagonal(pair_att[t][:], t, g), P_TOP, pt0_hi[r, heads, r],
                                ALU.mult, ALU.subtract)
                        lo.then_inc(pt0_ready, 1)
                if mid and not tail:
                    source_and_target(0)
                if mid and not tail:
                    h_low(1)
                if nxt:
                    low_part_transposed(0, i + 1, ht0_hi, ht0_lo, ht0_hi_ready, ht0_ready)
                if now:
                    for t in range(T):
                        dve.wait_ge(ct_hi_ready, 2 * i + t + 1)
                        nc.vector.scalar_tensor_tensor(ct_lo[:, t].rearrange("p k n -> p (k n)"), pair_att[t][:, 0:C],
                                                       1.0 / P_TOP, ct_hi[:, t].rearrange("p k n -> p (k n)"),
                                                       ALU.mult, ALU.subtract).then_inc(ct_ready, 1)
                if nxt:
                    low_part_transposed(1, i + 1, ht0_hi, ht0_lo, ht0_hi_ready, ht0_ready)
                if first:
                    largest(WL, 0)
                    largest(WL, 1)

                def keep_x1(t):
                    dve.wait_ge(bf_added, 2 * i + t + 1)
                    dve.wait_ge(f_psum, 2 * i + t + 1)
                    nc.vector.scalar_tensor_tensor(x1[:, t, :], pair_prj[t][:, 0:C], col(w_undo, WF), x1[:, t, :],
                                                   ALU.mult, ALU.add).then_inc(x1_ready, 1)

                def gate_argument(t):
                    dve.wait_ge(g_psum, 2 * j + t + 1)
                    nc.vector.scalar_tensor_tensor(gate[:, t, :], pair_prj[t][:, 0:C], col(w_undo, WG), bg_row[:],
                                                   ALU.mult, ALU.add).then_inc(g_ready, 1)

                def split_source_and_target():
                    whole = src_dst[:].rearrange("p t s a -> p (t s) a")
                    left = rest[:].rearrange("p t s a -> p (t s) a")
                    part = parts[:].rearrange("p t s (k a) -> p (t s) k a", k=3)
                    dve.wait_ge(src_ready, 2 * j + 2)
                    dve.wait_ge(dst_ready, 2 * j + 2)
                    nc.vector.tensor_copy(part[:, :, 0, :], whole).then_inc(part1_ready, 1)
                    dve.wait_ge(part1_ready, j + 1)
                    nc.vector.tensor_tensor(left, whole, part[:, :, 0, :], ALU.subtract).then_inc(rest_ready, 1)
                    dve.wait_ge(rest_ready, j + 1)
                    nc.vector.tensor_copy(part[:, :, 1, :], left).then_inc(part2_ready, 1)
                    dve.wait_ge(part2_ready, j + 1)
                    nc.vector.tensor_tensor(part[:, :, 2, :], left, part[:, :, 1, :], ALU.subtract)\
                        .then_inc(parts_ready, 1)

                def spread_over_heads(t):
                    dve.wait_ge(rhs_psum, 2 * j + t + 1)
                    rows_of = slice(0, 3 * PARTS1)
                    nc.vector.tensor_tensor(
                        logit_rhs[t].rearrange("p (a n) -> p a n", a=H1),
                        pair_att[t][rows_of, 512:512 + N].unsqueeze(1).broadcast_to([3 * PARTS1, H1, N]),
                        of_head[rows_of, :].unsqueeze(2).broadcast_to([3 * PARTS1, H1, N]), ALU.mult)\
                        .then_inc(logit_rhs_ready, 1)

                def mask_and_shift(t):
                    n = 2 * j + t + 1
                    dve.wait_ge(z_ready, n)
                    nc.vector.scalar_tensor_tensor(p1[:, t], p1[:, t], ALPHA, p1[:, t], ALU.mult, ALU.max)\
                        .then_inc(leaky_ready, 1)
                    after_alone(dve, eye_made, leaky_ready, n)
                    nc.vector.copy_predicated(p1[:, t], not_adj[:, t, :].unsqueeze(1).broadcast_to([P, H1, N]),
                                              neg_l1[:].unsqueeze(2).broadcast_to([P, H1, N])).then_inc(masked1, 1)
                    dve.wait_ge(masked1, n)
                    nc.vector.tensor_reduce(max1[:, t, :], p1[:, t], AX_X, ALU.max).then_inc(max1_ready, 1)
                    dve.wait_ge(max1_ready, n)
                    nc.vector.tensor_tensor(p1[:, t], p1[:, t], max1[:, t, :].unsqueeze(2).broadcast_to([P, H1, N]),
                                            ALU.subtract).then_inc(shifted1, 1)

                if mid:
                    source_and_target(1)
                    split_source_and_target()
                    gate_argument(0)
                    spread_over_heads(0)
                    spread_over_heads(1)
                    gate_argument(1)
                    after_alone(dve, eye_made, not_adj_made, j + 1)
                    mask_and_shift(0)
                before_tail = now and not nxt
                if now:
                    keep_x1(0)
                if before_tail:
                    dve.wait_ge(x1_ready, 2 * i + 1)
                    moments(1, x1, 0)
                if first:
                    scale_weight(WL)
                if mid:
                    mask_and_shift(1)
                if before_tail:
                    keep_x1(1)
                    dve.wait_ge(x1_ready, 2 * i + 2)
                    moments(1, x1, 1)
                    statistics(1, x1, i, begun=True)
                if mid:
                    sum_and_invert(0, j)
                if now and not before_tail:
                    keep_x1(1)
                if mid and not tail:
                    sum_and_invert(1, j)
                if now:
                    after(dve, masked1, 2 * j + 2)
                    nc.vector.tensor_scalar(not_adj[:], adj_u8[:], -1.0, 1.0, ALU.mult, ALU.add)\
                        .then_inc(not_adj_made, 1)
                if first:
                    scale_weight(WG)
                    dve.wait_ge(wf_ready, 2)
                    for half in range(2):
                        low_weight(WL, half)

            steps(dve, one)

        @block.scalar
        def _(act):
            def magnitudes(m, half):
                act.wait_ge(weight_loaded[m][half], DMA)
                nc.scalar.activation(w_hi[:, m, :, columns(half)], staging[m][:, :, columns(half)], ACT.Abs,
                                     accum_out=w_top[:, m, half:half + 1]).then_inc(weight_top[m], 1)

            def high_weight(m, half):
                act.wait_ge(weight_scaled, m + 1)
                nc.scalar.activation(w_hi[:, m, :, columns(half)], staging[m][:, :, columns(half)], ACT.Copy,
                                     scale=w_scale[:, m:m + 1]).then_inc(weight_hi, 1)

            def normalise(n, src, ready):
                for t in range(T):
                    nc.scalar.activation(rows[:, t, :], src[:, t, :], ACT.Relu, bias=shift[n][:, t:t + 1],
                                         scale=rstd[n][:, t:t + 1]).then_inc(ready, 1)

            def high_part_transposed(t, g, psum, hi_t, hi_ready):
                act.wait_ge(psum, 2 * g + t + 1)
                nc.scalar.activation(hi_t[:, :, t * P:(t + 1) * P],
                                     pair_prj[t][:, 0:C].rearrange("p (k n) -> p k n", k=KT), ACT.Copy)\
                    .then_inc(hi_ready, 1)

            def pt1_high(t, half, p, psum=pair_att):
                act.wait_ge(pt1_psum, 4 * p + 2 * t + half + 1)
                for g in range(2):
                    r = slice(N * g, N * g + N)
                    hi = nc.scalar.activation(
                        pt1_hi[r, heads_in(half, g), r], diagonal(psum[half][:], half, g), ACT.Copy, scale=P_TOP)
                hi.then_inc(pt1_hi_ready, 1)

            def exponentials1(t, g):
                act.wait_ge(shifted1, 2 * g + t + 1)
                nc.scalar.activation(p1[:, t], p1[:, t], ACT.Exp).then_inc(exp1_ready, 1)

            def h_from_kept(t, p):
                after(act, y_ready, 2 * p if is_late(t, p) else 2 * p + t)
                act.wait_ge(kept, p + 1)
                nc.scalar.activation(scratch(t, p)[2], keep[:, t, :], ACT.Relu, bias=keep_shift[:, t:t + 1],
                                     scale=keep_rstd[:, t:t + 1]).then_inc(h_again, 1)

            def output_exp(t, p):
                act.wait_ge(o_min, 2 * p + t + 1)
                nc.scalar.activation(scratch(t, p)[1], scratch(t, p)[1], ACT.Exp).then_inc(o_exp, 1)

            def output_parts(t, p):
                h_from_kept(t, p)
                output_exp(t, p)

            act.wait_ge(const_made, 6)
            nc.scalar.activation(keep_shift[:], minus_half[:], ACT.Abs)
            magnitudes(WQ, 0)
            act.wait_ge(shift_ready[0], 1)
            normalise(0, rows, rows0_ready)
            for t in range(T):
                high_part_transposed(t, 0, t0_psum, ht0_hi, ht0_hi_ready)
            for half in range(2):
                high_weight(WQ, half)
            for half in range(2):
                magnitudes(WK, half)
            for m in (WK, WV):
                for half in range(2):
                    high_weight(m, half)
            for half in range(2):
                magnitudes(WF, half)
            for half in range(2):
                high_weight(WF, half)
            for half in range(2):
                act.wait_ge(weight_hi, 2 * WF + half + 1)
                nc.scalar.activation(staging[WF][:, :, columns(half)], staging[WF][:, :, columns(half)], ACT.Copy,
                                     scale=w_scale[:, WF:WF + 1]).then_inc(wf_scaled, 1)

            def one(i, now, mid, last, nxt):
                j, p = i - 1, i - 2
                first = isinstance(i, int) and i == 0
                tail, final = mid and not now, last and not mid
                if isinstance(i, int) and i == 2:
                    act.wait_ge(pt1_cleared, 1)
                if tail:
                    pt1_high(0, 0, p)
                    pt1_high(0, 1, p)
                if mid:
                    act.wait_ge(shift_ready[1], j + 1)
                    act.wait_ge(t0_psum, 2 * i + 2 if now else 2 * GROUPS)
                    normalise(1, x1, rows1_ready)
                if last and not tail:
                    pt1_high(0, 0, p)
                    pt1_high(0, 1, p)
                    if final:
                        exponentials1(1, p)
                        h_from_kept(0, p)
                        h_from_kept(1, p)
                        act.wait_ge(o_psum, 2 * p + 1)
                        pt1_high(1, 0, p, pair_prj)
                        pt1_high(1, 1, p, pair_prj)
                        output_exp(0, p)
                        output_exp(1, p)
                    else:
                        output_parts(0, p)
                        pt1_high(1, 0, p)
                        pt1_high(1, 1, p)
                if mid:
                    if isinstance(i, int) and i == 1:
                        act.wait_ge(weight_ready, 2 * WG)
                    for t in range(T):
                        high_part_transposed(t, j, t1_psum, ht1_hi, ht1_hi_ready)
                if tail:
                    output_parts(0, p)
                    pt1_high(1, 0, p)
                    pt1_high(1, 1, p)
                    h_from_kept(1, p)
                elif last and not final:
                    output_parts(1, p)
                if now:
                    act.wait_ge(shifted0, i + 1)
                    nc.scalar.activation(p0, p0, ACT.Exp).then_inc(exp0_ready, 1)
                def high_values(t):
                    act.wait_ge(v_read, 2 * i + t + 1)
                    nc.scalar.activation(vals_hi[:, t, :], vals[:, t, :], ACT.Copy).then_inc(v_hi_ready, 1)

                if now:
                    high_values(0)
                    act.wait_ge(s_psum, 2 * i + 2)
                    nc.scalar.activation(units(21, 2), zero[:].broadcast_to([P, 2 * C]), ACT.Copy)\
                        .then_inc(pt0_cleared, 1)
                    if first:
                        act.wait_ge(shift_ready[0], i + 2)
                        normalise(0, rows, rows0_ready)
                    high_values(1)

                def h_high(t):
                    act.wait_ge(h_psum, 2 * j + t + 1)
                    nc.scalar.activation(h1v_hi[:, t, :], pair_prj[t][:, 0:C], ACT.Copy, scale=HV)

                def h_tanh(t):
                    if tail:
                        pass
                    elif t == 0:
                        after(act, diff_ready, 2 * p + 2)
                    else:
                        act.wait_ge(dst_prod, 2 * j + 1)
                    nc.scalar.activation(tanh_scratch(t, j)[0], pair_prj[t][:, 0:C], ACT.Tanh, scale=w_undo[:, WL:WL + 1])\
                        .then_inc(th_ready, 1)

                def probabilities_transposed(t):
                    act.wait_ge(pt0_psum, 2 * i + t + 1)
                    for g in range(2):
                        r = slice(N * g, N * g + N)
                        pt = nc.scalar.activation(pt0_hi[r, heads_in(t, g), r], diagonal(pair_att[t][:], t, g), ACT.Copy,
                                                  scale=P_TOP)
                    pt.then_inc(pt0_hi_ready, 1)

                if mid:
                    h_high(0)
                    h_tanh(0)
                    if tail:
                        output_exp(1, p)
                if nxt and not first:
                    act.wait_ge(shift_ready[0], i + 2)
                    normalise(0, rows, rows0_ready)
                if now:
                    act.wait_ge(pt0_cleared, i + 1)
                    for t in range(T):
                        probabilities_transposed(t)
                if mid:
                    h_high(1)
                    h_tanh(1)
                if nxt:
                    high_part_transposed(0, i + 1, t0_psum, ht0_hi, ht0_hi_ready)
                if now:
                    for t in range(T):
                        act.wait_ge(ct_psum, 2 * i + t + 1)
                        nc.scalar.activation(ct_hi[:, t].rearrange("p k n -> p (k n)"), pair_att[t][:, 0:C], ACT.Copy,
                                             scale=1.0 / P_TOP).then_inc(ct_hi_ready, 1)
                if nxt:
                    high_part_transposed(1, i + 1, t0_psum, ht0_hi, ht0_hi_ready)
                if first:
                    act.wait_ge(weight_ready, 2 * (WV + 1))
                    for half in range(2):
                        magnitudes(WG, half)
                if mid:
                    for t in range(T):
                        act.wait_ge(lhs_psum, 2 * j + t + 1)
                        nc.scalar.activation(logit_lhs[0:PARTS1, t, :], pair_att[t][0:PARTS1, 0:P], ACT.Copy)\
                            .then_inc(logit_lhs_ready, 1)
                    for t in range(T):
                        act.wait_ge(z_psum, 2 * j + t + 1)
                        nc.scalar.activation(p1[:, t], pair_att[t][:, 0:C].rearrange("p (a n) -> p a n", a=H1), ACT.Copy)\
                            .then_inc(z_ready, 1)
                    for t in range(T):
                        act.wait_ge(g_ready, 2 * j + t + 1)
                        nc.scalar.activation(gate[:, t, :], gate[:, t, :], ACT.Tanh, scale=0.5).then_inc(gate_ready, 1)
                    exponentials1(0, j)
                    if not tail:
                        exponentials1(1, j)
                if first:
                    for m in (WL, WG):
                        for half in range(2):
                            high_weight(m, half)

            steps(act, one)

        @block.gpsimd
        def _(pool):
            nc.gpsimd.memset(ident[:], 0.0).then_inc(eye_cleared, 1)
            pool.wait_ge(eye_cleared, 1)
            nc.gpsimd.affine_select(out=ident[:], in_=ident[:], compare_op=ALU.not_equal, fill=1.0, base=0,
                                    pattern=[[-1, P]], channel_multiplier=1).then_inc(eye_made, 1)
            nc.gpsimd.memset(in_graph[:], 0.0).then_inc(eye_cleared, 1)
            nc.gpsimd.memset(neg_l1[:], NEG_L1).then_inc(const_made, 1)
            nc.gpsimd.memset(minus_half[:], -0.5).then_inc(const_made, 1)
            nc.gpsimd.memset(zero[:], 0.0).then_inc(const_made, 1)
            nc.gpsimd.memset(to_true[:], 1.0 / HN).then_inc(const_made, 1)
            pool.wait_ge(eye_cleared, 2)
            for g in range(2):
                pool.wait_ge(const_made, 4 + g)
                nc.gpsimd.memset(in_graph[N * g:N * g + N, g:g + 1], 1.0).then_inc(const_made, 1)
            pool.wait_ge(const_made, 6)
            nc.gpsimd.memset(p0_place[:], 0.0).then_inc(eye_cleared, 1)
            nc.gpsimd.memset(p1_place[:], 0.0).then_inc(eye_cleared, 1)
            pool.wait_ge(eye_made, 1)
            nc.gpsimd.tensor_tensor(node_eye[:], ident[:, 0:N], ident[:, N:P], ALU.add).then_inc(eye_made, 1)
            pool.wait_ge(const_made, 6)

            def top_weight(m):
                pool.wait_ge(weight_top[m], 2)
                nc.gpsimd.partition_all_reduce(w_all[:, m], w_top[:, m], P, MAX_OVER_PARTITIONS)\
                    .then_inc(weight_all, 1)

            def power(n, g):
                pool.wait_ge(var_ready[n], g + 1)
                nc.gpsimd.tensor_tensor(rstd[n][:], var_eps[n][:], minus_half[:], ALU.pow).then_inc(rstd_ready[n], 1)

            power(0, 0)
            for m in (WQ, WK, WV, WF):
                top_weight(m)
            pool.wait_ge(eye_made, 2)
            pool.wait_ge(const_loaded, 6 * DMA)
            power(0, 1)
            for half in range(2):
                pool.wait_ge(wf_scaled, half + 1)
                nc.gpsimd.tensor_tensor(w_lo[:, WF, :, columns(half)], staging[WF][:, :, columns(half)],
                                        w_hi[:, WF, :, columns(half)], ALU.subtract).then_inc(wf_ready, 1)

            def one(i, now, mid, last, nxt):
                j, p = i - 1, i - 2
                first = isinstance(i, int) and i == 0
                tail, final = mid and not now, last and not mid
                if isinstance(i, int) and i == 1:
                    power(1, j)
                    pool.wait_ge(weight_ready, 2 * WG)
                    nc.gpsimd.memset(units(7, 2), 0.0).then_inc(pt1_cleared, 1)
                elif mid and not tail:
                    power(1, j)

                def add_bias(t):
                    pool.wait_ge(o_norm, 2 * p + t + 1)
                    o = scratch(t, p)[0].rearrange("p (a n) -> p a n", a=H1)
                    nc.gpsimd.tensor_tensor(o, o, b1_row[:].unsqueeze(1).broadcast_to([P, H1, E1]), ALU.add)\
                        .then_inc(o_biased, 1)

                def add_h(t):
                    pool.wait_ge(summed, 2 * p + t + 1)
                    nc.gpsimd.tensor_tensor(keep[:, t, :], keep[:, t, :], scratch(t, p)[2], ALU.add)\
                        .then_inc(y_ready, 1)

                def keep_copy():
                    after(pool, out_stored, 2 * DMA * j)
                    after(pool, rows1_ready, 2 * j + 2)
                    both = to_true[:].broadcast_to([P, T])
                    nc.gpsimd.tensor_tensor(keep_rstd[:], rstd[1][:], both, ALU.mult)
                    nc.gpsimd.tensor_tensor(keep_shift[:], shift[1][:], both, ALU.mult)
                    nc.gpsimd.tensor_copy(keep, x1).then_inc(kept, 1)

                def products(t):
                    th, by_src, by_dst = tanh_scratch(t, j)
                    pool.wait_ge(th_ready, 2 * j + t + 1)
                    if tail:
                        pool.wait_ge(y_ready, 2 * p + 1)
                    elif t == 0:
                        after(pool, summed, 2 * p + 2)
                    else:
                        pool.wait_ge(dst_ready, 2 * j + 1)
                    nc.gpsimd.tensor_tensor(by_src, th, src_row[:], ALU.mult).then_inc(src_prod, 1)
                    nc.gpsimd.tensor_tensor(by_dst, th, dst_row[:], ALU.mult).then_inc(dst_prod, 1)

                if final:
                    add_bias(0)
                    add_bias(1)
                    add_h(0)
                    add_h(1)
                elif tail:
                    add_bias(0)
                    add_h(0)
                    add_bias(1)
                    products(0)
                    products(1)
                    add_h(1)
                elif last:
                    for t in range(T):
                        add_bias(t)
                        add_h(t)
                if mid and not tail:
                    keep_copy()
                if nxt and not first:
                    power(0, i + 1)
                if mid and not tail:
                    products(0)
                    products(1)
                if mid:
                    pool.wait_ge(parts_ready, j + 1)
                    shape = [P, T, 2, PARTS1]
                    nc.gpsimd.tensor_tensor(
                        dst_terms[:, :, PARTS1:].rearrange("p t (g q) -> p t g q", g=2),
                        parts[:, :, 1, :].unsqueeze(2).broadcast_to(shape),
                        in_graph[:].unsqueeze(1).unsqueeze(3).broadcast_to(shape), ALU.mult)\
                        .then_inc(dst_terms_ready, 1)
                    if tail:
                        keep_copy()
                if now:
                    pool.wait_ge(x1_loaded, DMA * (i + 1))
                    for t in range(T):
                        nc.gpsimd.tensor_tensor(x1[:, t, :], x1[:, t, :], bf_row[:], ALU.add).then_inc(bf_added, 1)
                if now and not nxt:
                    power(1, i)
                if first:
                    top_weight(WL)
                    top_weight(WG)

            steps(pool, one)


_INS = ['x', 'adj', 'L0_gnn_Wq', 'L0_gnn_bq', 'L0_gnn_Wk', 'L0_gnn_bk', 'L0_gnn_Wv', 'L0_gnn_bv', 'L0_gnn_Wf',
        'L0_gnn_bf', 'L1_gnn_W', 'L1_gnn_b', 'L1_gnn_w_src', 'L1_gnn_w_dst', 'L1_gnn_H_w', 'L1_gnn_H_b']


def kernel(**inputs):
    import concourse.bacc as bacc
    from concourse.bass_utils import run_bass_kernel_spmd

    arrays = {name: np.ascontiguousarray(inputs[name]) for name in _INS}

    for name in ('L0_gnn_bq', 'L0_gnn_bk'):
        arrays[name] = np.ascontiguousarray(arrays[name].reshape(-1, P).T)
    heads, features, width = arrays['L1_gnn_W'].shape
    arrays['L1_gnn_W'] = np.ascontiguousarray(arrays['L1_gnn_W'].transpose(1, 0, 2).reshape(features, heads * width))
    arrays['L1_gnn_H_w'] = np.ascontiguousarray(arrays['L1_gnn_H_w'].T)

    nc = bacc.Bacc("TRN2", target_bir_lowering=False, num_devices=1)
    args = [nc.dram_tensor(f"in_{n}", arrays[n].shape, mybir.dt.from_np(arrays[n].dtype), kind="ExternalInput").ap()
            for n in _INS]
    out = nc.dram_tensor("out_0", arrays['x'].shape, F32, kind="ExternalOutput").ap()
    build_two_layer_gnn(nc, *args, out)
    r = run_bass_kernel_spmd(nc, [{f"in_{n}": arrays[n] for n in _INS}], core_ids=[0])
    return r.results[0]["out_0"]
```
